# Optimizing a Trainium2 kernel written in Bass

```python
import numpy as np
import jax
import jax.numpy as jnp

def _softmax(x, axis=-1):
    return jax.nn.softmax(x, axis=axis)

def _gelu(x):
    return jax.nn.gelu(x, approximate=True)

def _silu(x):
    return jax.nn.silu(x)

def _sigmoid(x):
    return jax.nn.sigmoid(x)

def _layernorm(x, axis=-1, eps=1e-05):
    m = jnp.mean(x, axis=axis, keepdims=True)
    v = jnp.var(x, axis=axis, keepdims=True)
    return (x - m) / jnp.sqrt(v + eps)

def _scatter_add(tgt, idx, src, axis=0):
    return tgt.at[idx].add(src)

def _segment_sum(src, seg, n):
    return jax.ops.segment_sum(src, seg, n)
kernel_name = 'mk_adj_preln_d1_adj_r2_8ef8c2'

def setup_inputs(seed: int=0):
    np.random.seed(seed)
    _w = jnp.asarray

    def _rec_inputs():
        import jax
        import jax.numpy as jnp
        _gk = jax.random.key(seed)
        x = 7.22e-05 + 1 * jax.random.normal(jax.random.fold_in(_gk, 1), (32, 256, 128), jnp.float32)
        _a = jax.random.bernoulli(jax.random.fold_in(_gk, 2), 0.0078125, (32, 256, 256))
        _af = _a.astype(jnp.float32)
        adj = _af
        _nm = jnp.ones((32, 256), dtype=bool)
        nodemask = jnp.where(_nm, 1.0, 0.0).astype(jnp.float32)
        return (x, adj, nodemask)
    x, adj, nodemask = _rec_inputs()

    def _L0_gnn_setup():
        import jax, jax.numpy as jnp
        import numpy as np
        B, N, D, C, L = (64, 256, 128, 128, 5)
        EDGE_P = 0.02

        def _gru_cell(m, h, w_ih, w_hh, b_ih, b_hh):
            gi = m @ w_ih.T + b_ih
            gh = h @ w_hh.T + b_hh
            i_r, i_z, i_n = jnp.split(gi, 3, axis=-1)
            h_r, h_z, h_n = jnp.split(gh, 3, axis=-1)
            r = jax.nn.sigmoid(i_r + h_r)
            z = jax.nn.sigmoid(i_z + h_z)
            n = jnp.tanh(i_n + r * h_n)
            return (1.0 - z) * n + z * h
        key = jax.random.key(seed)
        ks = jax.random.split(key, 8)
        x = jax.random.normal(ks[0], (B, N, D), dtype=jnp.float32)
        adj = (jax.random.uniform(ks[1], (B, N, N)) < EDGE_P).astype(jnp.float32)
        mask = jnp.ones((B, N), dtype=jnp.float32)
        s = 1.0 / np.sqrt(C).astype(np.float32)
        weight = jax.random.uniform(ks[2], (L, C, C), minval=-s, maxval=s, dtype=jnp.float32)
        w_ih = jax.random.uniform(ks[3], (3 * C, C), minval=-s, maxval=s, dtype=jnp.float32)
        w_hh = jax.random.uniform(ks[4], (3 * C, C), minval=-s, maxval=s, dtype=jnp.float32)
        b_ih = jax.random.uniform(ks[5], (3 * C,), minval=-s, maxval=s, dtype=jnp.float32)
        b_hh = jax.random.uniform(ks[6], (3 * C,), minval=-s, maxval=s, dtype=jnp.float32)
        return dict(x=x, adj=adj, mask=mask, weight=weight, w_ih=w_ih, w_hh=w_hh, b_ih=b_ih, b_hh=b_hh)
    _L0_gnn_all = _L0_gnn_setup()
    _L0_gnn_in = {k: v for k, v in _L0_gnn_all.items() if k in ('weight', 'w_ih', 'w_hh', 'b_ih', 'b_hh')}
    del _L0_gnn_all
    return {'x': x, 'adj': adj, 'nodemask': nodemask, 'L0_gnn_weight': _L0_gnn_in['weight'], 'L0_gnn_w_ih': _L0_gnn_in['w_ih'], 'L0_gnn_w_hh': _L0_gnn_in['w_hh'], 'L0_gnn_b_ih': _L0_gnn_in['b_ih'], 'L0_gnn_b_hh': _L0_gnn_in['b_hh']}

def reference(x, adj, nodemask, L0_gnn_weight, L0_gnn_w_ih, L0_gnn_w_hh, L0_gnn_b_ih, L0_gnn_b_hh):
    import jax
    import jax.numpy as jnp

    def _L0_gnn_ref(x, adj, mask, weight, w_ih, w_hh, b_ih, b_hh):
        import jax, jax.numpy as jnp
        import numpy as np
        B, N, D, C, L = (64, 256, 128, 128, 5)
        EDGE_P = 0.02

        def _gru_cell(m, h, w_ih, w_hh, b_ih, b_hh):
            gi = m @ w_ih.T + b_ih
            gh = h @ w_hh.T + b_hh
            i_r, i_z, i_n = jnp.split(gi, 3, axis=-1)
            h_r, h_z, h_n = jnp.split(gh, 3, axis=-1)
            r = jax.nn.sigmoid(i_r + h_r)
            z = jax.nn.sigmoid(i_z + h_z)
            n = jnp.tanh(i_n + r * h_n)
            return (1.0 - z) * n + z * h
        A = (adj != 0).astype(x.dtype)
        h = x
        for l in range(weight.shape[0]):
            m = jnp.einsum('bnd,de->bne', h, weight[l])
            agg = jnp.einsum('bij,bid->bjd', A, m)
            h = _gru_cell(agg, h, w_ih, w_hh, b_ih, b_hh)
        return h * mask[..., None]
    h = jnp.maximum(_layernorm(x, axis=-1), 0.0)
    x = x + _L0_gnn_ref(h, adj, nodemask, L0_gnn_weight, L0_gnn_w_ih, L0_gnn_w_hh, L0_gnn_b_ih, L0_gnn_b_hh)
    return x

_drawn_inputs = setup_inputs


def setup_inputs(seed=0):
    import zlib

    import numpy as np

    out = dict(_drawn_inputs(seed))
    spreads = {}
    factors = {}
    for name, (base, spread) in spreads.items():
        noise = np.random.default_rng([zlib.crc32(name.encode()), seed]).standard_normal(out[name].shape)
        drawn = base * np.exp(spread * noise) if base else spread * noise
        out[name] = jnp.asarray(drawn.astype(out[name].dtype))
    for name, factor in factors.items():
        out[name] = (out[name] * factor).astype(out[name].dtype)
    return out
```

```python
from contextlib import ExitStack

import concourse.bass as bass
from concourse import mybir

FP32 = mybir.dt.float32
FP16 = mybir.dt.float16
I32 = mybir.dt.int32
ALU = mybir.AluOpType
ACT = mybir.ActivationFunctionType
AX = mybir.AxisListType

B, N, D, L = 32, 256, 128, 5
G3 = 3 * D
PAIRS = B // 2
COLS = 2 * N
LOG_PAIRS = PAIRS.bit_length() - 1
CH = COLS // 128
STEPS = L * PAIRS
LAST = STEPS - PAIRS
EPS = 1e-5

S_H = 256.0
S_A = 1.0 / 16.0
S_AGG = S_H * S_A
S_V = 2.0 ** 14


def gnn_program(nc, x, adj, nodemask, weight, w_ih, w_hh, b_ih, b_hh, out):
    x_v = x.rearrange("(t b) (k q) d -> t q (b k) d", b=2, q=128)
    adj_v = adj.rearrange("(t b) (k q) j -> t q (b k) j", b=2, q=128)
    out_v = out.rearrange("(t b) (k q) d -> t q (b k) d", b=2, q=128)
    mask_v = nodemask.rearrange("b (k q) -> (b k) q", q=128)

    ctx = ExitStack()
    with ctx:
        def sb(name, shape, dt):
            return ctx.enter_context(nc.sbuf_tensor(name, shape, dt))

        def pb(name, shape, dt=FP32):
            return ctx.enter_context(nc.psum_tensor(name, shape, dt))

        def sem(name):
            return ctx.enter_context(nc.semaphore(name))

        xs = sb("xs", [128, PAIRS, CH, D], FP32)
        h = sb("h", [128, PAIRS, COLS], FP32)
        hT = sb("hT", [128, PAIRS, 2, COLS], FP16)
        hN = sb("hN", [128, PAIRS, CH, 2, D], FP16)
        A = sb("A", [128, PAIRS, CH, N], FP16)
        VT = sb("VT", [128, L, 2, G3], FP16)
        WT = sb("WT", [128, 2, G3], FP16)
        ident = sb("ident", [128, 128], FP32)
        ident16 = sb("ident16", [128, 128], FP16)
        ones_row = sb("ones_row", [1, 128], FP32)
        minus_half = sb("minus_half", [128, CH], FP32)
        eps = sb("eps", [128, CH], FP32)
        rows = sb("rows", [70, 128], FP32)
        mask_t = sb("mask_t", [128, 2 * B], FP32)
        bias = sb("bias", [128, 6], FP32)
        bias_r = sb("bias_r", [128, 1], FP32)
        bias_z = sb("bias_z", [128, 1], FP32)
        bias_hn = sb("bias_hn", [128, 1], FP32)
        w_max = sb("w_max", [128, 2], FP32)
        top = sb("top", [1, 4], FP32)
        scales = sb("scales", [128, 3], FP32)
        adj_in = [sb(f"adj_in{i}", [128, CH, N], FP32) for i in range(2)]
        stats = [sb(f"stats{i}", [128, CH, 6], FP32) for i in range(2)]
        moments = [sb(f"moments{i}", [128, CH, 2], FP32) for i in range(2)]
        var_eps = [sb(f"var_eps{i}", [128, CH], FP32) for i in range(2)]
        rstd = [sb(f"rstd{i}", [128, CH], FP32) for i in range(2)]
        xn = [sb(f"xn{i}", [128, CH, D], FP32) for i in range(2)]
        agg = [sb(f"agg{i}", [128, 2, COLS], FP16) for i in range(2)]
        ru = [sb(f"ru{i}", [128, COLS], FP32) for i in range(2)]
        z = [sb(f"z{i}", [128, COLS], FP32) for i in range(2)]
        n = [sb(f"n{i}", [128, COLS], FP32) for i in range(2)]
        zh = [sb(f"zh{i}", [128, COLS], FP32) for i in range(2)]
        raw = h[:, 8:PAIRS, :].rearrange("p a c -> p (a c)")
        w_raw = raw[:, 0:640].rearrange("p (l e) -> p l e", l=L)
        ih_raw = raw[:, 640:1024].rearrange("p (g e) -> p g e", g=3)
        hh_raw = raw[:, 1024:1408].rearrange("p (g e) -> p g e", g=3)
        ihT = raw[:, 1408:1792]
        wlT = raw[:, 1792:2432].rearrange("p (l d) -> p l d", l=L)
        raw2 = hT[:, 8:PAIRS, :, :].rearrange("p a t c -> p (a t c)").bitcast(FP32)
        vf = raw2[:, 0:L * G3].rearrange("p (l f) -> p l f", l=L)
        wf = raw2[:, L * G3:(L + 1) * G3]
        h_end = [adj_in[i][:, 0:2, :].rearrange("p a c -> p (a c)") for i in range(2)]
        y = [adj_in[i][:, 2:4, :].rearrange("p a c -> p (a c)") for i in range(2)]

        p_r = pb("p_r", [128, COLS])
        p_z = pb("p_z", [128, COLS])
        p_in = pb("p_in", [128, COLS])
        p_hn = pb("p_hn", [128, COLS])
        p_agg = pb("p_agg", [128, COLS])
        p_tr = pb("p_tr", [128, CH, 2, D], FP16)
        p_tp = pb("p_tp", [128, CH, 2, D], FP16)
        p_x = pb("p_x", [128, COLS])
        v_banks = [p_r, p_z, p_in, p_agg, p_tr[:, :, :, :].rearrange("p c t d -> p (c t d)").bitcast(FP32)]

        s_small_in = sem("small_in")
        s_w_in = [sem(f"w_in{i}") for i in range(3)]
        s_x_in = [sem(f"x_in{i}") for i in range(2)]
        s_adj_in = [sem(f"adj_in_sem{i}") for i in range(2)]
        s_out = [sem(f"out_sent{i}") for i in range(2)]
        s_pool_own = sem("pool_own")
        s_ident = sem("ident_ready")
        s_ones = sem("ones_ready")
        s_dve_own = sem("dve_own")
        s_pe_setup = sem("pe_setup")
        s_setup_used = sem("setup_used")
        s_weights = sem("weights_ready")
        s_bias = sem("bias_ready")
        s_stats_own = sem("stats_own")
        s_moments = sem("moments_ready")
        s_var = sem("var_eps_ready")
        s_rstd = sem("rstd_ready")
        s_xn = sem("xn_ready")
        s_tx = sem("tx_done")
        s_h0hi = sem("h0_hi_ready")
        s_h0lo = sem("h0_lo_ready")
        s_tp = sem("tp_done")
        s_hn0 = sem("hn0_ready")
        s_a = sem("a_ready")
        s_agg = sem("agg_done")
        s_agghi = sem("agg_hi_ready")
        s_agglo = sem("agg_lo_ready")
        s_pr = sem("p_r_done")
        s_pz = sem("p_z_done")
        s_pin = sem("p_in_done")
        s_r = sem("r_ready")
        s_z = sem("z_ready")
        s_t = sem("t_ready")
        s_u = sem("u_ready")
        s_n = sem("n_ready")
        s_v = sem("v_own")
        s_zh = sem("zh_ready")
        s_hnew = sem("h_new_ready")
        s_hi = sem("hi_ready")
        s_lo = sem("lo_ready")
        s_tr = sem("tr_done")
        s_hn = sem("hN_ready")
        s_ty = sem("ty_done")
        s_ym = sem("y_masked")
        s_y = sem("y_ready")

        block = ctx.enter_context(nc.Block())

        OWN_MAX, OWN_TOP, OWN_SCALES = 4, 9, 10

        def wait(eng, s, count):
            if isinstance(count, int) and count <= 0:
                return
            eng.wait_ge(s, count)

        def slot(s):
            return s % PAIRS if isinstance(s, int) else s & (PAIRS - 1)

        def half(s):
            return s >> 1

        def run(eng, step):
            for s in range(-4, 4):
                step(s, s)
            with eng.Fori(2, 6) as i:
                for k in range(2):
                    step(i * 2 + k, 4 + k)
            for s in range(12, 16):
                step(s, s)
            with eng.Fori(8, LAST // 2) as i:
                for k in range(2):
                    step(i * 2 + k, 16 + k)
            for s in range(LAST, LAST + 4):
                step(s, s)
            with eng.Fori(LAST // 2 + 2, STEPS // 2 - 1) as i:
                for k in range(2):
                    step(i * 2 + k, LAST + 4 + k)
            for s in range(STEPS - 2, STEPS + 3):
                step(s, s)

        def first(k):
            return 0 <= k < PAIRS

        def inner(k):
            return 0 <= k < LAST

        def end(k):
            return LAST <= k < STEPS

        def real(k):
            return 0 <= k < STEPS

        @block.sync
        def _(sp):
            sp.dma_start(ih_raw, w_ih.rearrange("(g f) e -> f g e", g=3)).then_inc(s_w_in[0], 16)
            sp.dma_start(w_raw, weight.rearrange("l d e -> d l e")).then_inc(s_w_in[2], 16)
            sp.dma_start(hh_raw, w_hh.rearrange("(g f) e -> f g e", g=3)).then_inc(s_w_in[1], 16)

            def load(q, k):
                pair = nc.s_assert_within(q, 0, PAIRS - 1, skip_runtime_bounds_check_because="the loop ends there")
                wait(sp, s_moments, q - 1)
                sp.dma_start(xs[:, pair, :, :], x_v[pair]).then_inc(s_x_in[k % 2], 16)
                wait(sp, s_a, q - 1)
                sp.dma_start(adj_in[k % 2][:, :, :], adj_v[pair]).then_inc(s_adj_in[k % 2], 16)

            for q in range(2):
                load(q, q)
            with sp.Fori(1, PAIRS // 2) as i:
                for k in range(2):
                    load(i * 2 + k, k)

            def store(o, k):
                pair = nc.s_assert_within(o, 0, PAIRS - 1, skip_runtime_bounds_check_because="the loop ends there")
                wait(sp, s_y, o + 1)
                sp.dma_start(out_v[pair], y[k % 2].rearrange("p (c d) -> p c d", c=CH)).then_inc(s_out[k % 2], 16)

            with sp.Fori(0, PAIRS // 2) as i:
                for k in range(2):
                    store(i * 2 + k, k)
            for k in range(2):
                sp.wait_ge(s_out[k], 16 * (PAIRS // 2))

        @block.tensor
        def _(pe):
            pe.wait_ge(s_ident, 2)
            pe.wait_ge(s_w_in[0], 16)
            for g in range(3):
                t = nc.tensor.transpose(p_r[:, g * D:(g + 1) * D], ih_raw[:, g, :], ident[:, :])
            t.then_inc(s_pe_setup, 1)
            pe.wait_ge(s_w_in[2], 16)
            for l in range(L):
                bank = p_z if l < 4 else p_in
                c = (l % 4) * D
                t = nc.tensor.transpose(bank[:, c:c + D], w_raw[:, l, :], ident[:, :])
            t.then_inc(s_pe_setup, 1)
            pe.wait_ge(s_w_in[1], 16)
            for g in range(3):
                t = nc.tensor.transpose(p_hn[:, g * D:(g + 1) * D], hh_raw[:, g, :], ident[:, :])
            t.then_inc(s_pe_setup, 1)
            pe.wait_ge(s_small_in, 48)
            nc.tensor.transpose(p_x[:, 0:70], rows[:, :], ident[0:70, 0:70]).then_inc(s_pe_setup, 1)
            pe.wait_ge(s_setup_used, 2)
            for l in range(L):
                nc.tensor.matmul(v_banks[l][:, 0:G3], wlT[:, l, :], ihT[:, :], start=True, stop=True
                                 ).then_inc(s_pe_setup, 1)
            pe.wait_ge(s_dve_own, OWN_MAX)
            nc.tensor.transpose(p_hn[0:1, 384:512], w_max[:, 0:1], ident[:, :]).then_inc(s_pe_setup, 1)
            pe.wait_ge(s_ones, 1)
            pe.wait_ge(s_dve_own, OWN_TOP)
            nc.tensor.matmul(p_hn[:, 384:387], ones_row[0:1, :], top[0:1, 0:3], start=True, stop=True
                             ).then_inc(s_pe_setup, 1)

            def step(s, k):
                if first(k + 3):
                    q = s + 3
                    wait(pe, s_xn, q + 1)
                    wait(pe, s_h0hi, q)
                    if k + 3 == 0:
                        pe.wait_ge(s_bias, 1)
                    for c in range(CH):
                        t = nc.tensor.transpose(p_x[:, c * 128:(c + 1) * 128], xn[(k + 3) % 2][:, c, :], ident[:, :])
                    t.then_inc(s_tx, 1)
                if inner(k - 3):
                    o = s - 3
                    wait(pe, s_hi, o + 1)
                    wait(pe, s_lo, o + 1)
                    wait(pe, s_hn, o)
                    for c in range(CH):
                        for part in range(2):
                            t = nc.tensor.transpose(p_tr[:, c, part, :], hT[:, slot(o), part, c * 128:(c + 1) * 128],
                                                    ident16[:, :])
                    t.then_inc(s_tr, 1)
                if end(k - 2):
                    o = s - 2 - LAST
                    wait(pe, s_hnew, o + LAST + 1)
                    wait(pe, s_ym, o)
                    for c in range(CH):
                        t = nc.tensor.transpose(p_x[:, c * 128:(c + 1) * 128],
                                                h_end[k % 2][:, c * 128:(c + 1) * 128], ident[:, :])
                    t.then_inc(s_ty, 1)
                if real(k + 1):
                    a = s + 1
                    if first(k + 1):
                        wait(pe, s_hn0, a + 1)
                        wait(pe, s_a, a + 1)
                        if k + 1 == 0:
                            pe.wait_ge(s_weights, 1)
                    else:
                        wait(pe, s_hn, a + 1 - PAIRS)
                    wait(pe, s_agglo, a)
                    for b in range(2):
                        for m in range(4):
                            half, part = m // 2, m % 2
                            t = nc.tensor.matmul(p_agg[:, b * N:(b + 1) * N], hN[:, slot(a), 2 * b + half, part, :],
                                                 A[:, slot(a), 2 * b + half, :], start=(m == 0), stop=(m == 3))
                    t.then_inc(s_agg, 1)
                if first(k + 2):
                    q = s + 2
                    wait(pe, s_h0hi, q + 1)
                    wait(pe, s_h0lo, q + 1)
                    wait(pe, s_hn0, q)
                    for c in range(CH):
                        for part in range(2):
                            t = nc.tensor.transpose(p_tp[:, c, part, :], hT[:, slot(q), part, c * 128:(c + 1) * 128],
                                                    ident16[:, :])
                    t.then_inc(s_tp, 1)
                if real(k):
                    middle = PAIRS <= k < LAST
                    layer = (s >> LOG_PAIRS) if middle else k // PAIRS
                    hi, lo = hT[:, slot(s), 0, :], hT[:, slot(s), 1, :]
                    ahi, alo = agg[k % 2][:, 0, :], agg[k % 2][:, 1, :]

                    def products(bank, gate, table, data, start, stop):
                        c = gate * D
                        nc.tensor.matmul(bank[:, :], table[:, 0, c:c + D], data[0], start=start, stop=False)
                        nc.tensor.matmul(bank[:, :], table[:, 0, c:c + D], data[1], start=False, stop=False)
                        return nc.tensor.matmul(bank[:, :], table[:, 1, c:c + D], data[0], start=False, stop=stop)

                    V = VT[:, layer, :, :]
                    wait(pe, s_t, s)
                    products(p_hn, 2, WT, (hi, lo), True, True)
                    wait(pe, s_r, s)
                    products(p_r, 0, WT, (hi, lo), True, False)
                    wait(pe, s_agglo, s + 1)
                    products(p_r, 0, V, (ahi, alo), False, True).then_inc(s_pr, 1)
                    wait(pe, s_z, s)
                    products(p_z, 1, WT, (hi, lo), True, False)
                    products(p_z, 1, V, (ahi, alo), False, True).then_inc(s_pz, 1)
                    wait(pe, s_u, s)
                    products(p_in, 2, V, (ahi, alo), True, True).then_inc(s_pin, 1)

            run(pe, step)

        @block.scalar
        def _(act):
            act.dma_start(rows[0:64, :], mask_v).then_inc(s_small_in, 16)
            act.dma_start(rows[64:67, :], b_ih.rearrange("(g f) -> g f", g=3)).then_inc(s_small_in, 16)
            act.dma_start(rows[67:70, :], b_hh.rearrange("(g f) -> g f", g=3)).then_inc(s_small_in, 16)
            act.wait_ge(s_pe_setup, 1)
            nc.scalar.activation(ihT[:, :], p_r[:, 0:G3], ACT.Copy).then_inc(s_setup_used, 1)
            act.wait_ge(s_pe_setup, 2)
            nc.scalar.activation(wlT[:, 0:4, :].rearrange("p l d -> p (l d)"), p_z[:, :], ACT.Copy)
            nc.scalar.activation(wlT[:, 4, :], p_in[:, 0:D], ACT.Copy).then_inc(s_setup_used, 1)
            for l in range(L):
                act.wait_ge(s_pe_setup, 5 + l)
                nc.scalar.activation(vf[:, l, :], v_banks[l][:, 0:G3], ACT.Copy).then_inc(s_setup_used, 1)
            act.wait_ge(s_dve_own, OWN_SCALES)
            act.wait_ge(s_setup_used, 7)
            nc.scalar.activation(VT[:, :, 0, :], vf[:, :, :], ACT.Copy, scale=scales[:, 0:1])
            nc.scalar.activation(WT[:, 0, :], wf[:, :], ACT.Copy, scale=scales[:, 1:2]).then_inc(s_setup_used, 1)

            def step(s, k):
                if inner(k - 2):
                    o = s - 2
                    wait(act, s_hnew, o + 1)
                    nc.scalar.activation(hT[:, slot(o), 0, :], h[:, slot(o), :], ACT.Copy).then_inc(s_hi, 1)
                if real(k - 1):
                    o = s - 1
                    wait(act, s_u, o + 1)
                    if k == 1:
                        act.wait_ge(s_bias, 2)
                    nc.scalar.activation(n[(k - 1) % 2][:, :], ru[(k - 1) % 2][:, :], ACT.Tanh,
                                         bias=bias[:, 2:3], scale=scales[:, 2:3]).then_inc(s_n, 1)
                if first(k + 3):
                    q = s + 3
                    wait(act, s_tx, q + 1)
                    nc.scalar.activation(h[:, slot(q), :], p_x[:, :], ACT.Relu, scale=S_H)
                    nc.scalar.activation(hT[:, slot(q), 0, :], p_x[:, :], ACT.Relu, scale=S_H).then_inc(s_h0hi, 1)
                if real(k + 1):
                    a = s + 1
                    wait(act, s_agg, a + 1)
                    wait(act, s_pin, a - 1)
                    nc.scalar.activation(agg[(k + 1) % 2][:, 0, :], p_agg[:, :], ACT.Copy).then_inc(s_agghi, 1)
                if first(k + 2):
                    q = s + 2
                    wait(act, s_tp, q + 1)
                    nc.scalar.activation(hN[:, slot(q), :, :, :], p_tp[:, :, :, :], ACT.Copy).then_inc(s_hn0, 1)
                if real(k):
                    wait(act, s_pr, s + 1)
                    if k == 0:
                        act.wait_ge(s_bias, 2)
                    wait(act, s_n, s - 1)
                    nc.scalar.activation(ru[k % 2][:, :], p_r[:, :], ACT.Sigmoid, bias=bias_r[:, :],
                                         scale=scales[:, 2:3]).then_inc(s_r, 1)
                    wait(act, s_pz, s + 1)
                    wait(act, s_hnew, s - 1)
                    nc.scalar.activation(z[k % 2][:, :], p_z[:, :], ACT.Sigmoid, bias=bias_z[:, :],
                                         scale=scales[:, 2:3]).then_inc(s_z, 1)

            run(act, step)

        @block.vector
        def _(dve):
            own = [0]

            def chained(ins):
                own[0] += 1
                ins.then_inc(s_dve_own, 1)
                dve.wait_ge(s_dve_own, own[0])

            def setup():
                nc.vector.memset(ones_row[:, :], 1.0).then_inc(s_ones, 1)
                dve.wait_ge(s_pe_setup, 3)
                nc.vector.tensor_copy(wf[:, :], p_hn[:, 0:G3]).then_inc(s_dve_own, 1)
                own[0] += 1
                dve.wait_ge(s_pe_setup, 4)
                nc.vector.tensor_scalar(mask_t[:, :], p_x[:, 0:64], 1.0 / S_H, None, ALU.mult)
                chained(nc.vector.tensor_copy(bias[:, :], p_x[:, 64:70]))
                nc.vector.tensor_tensor(bias_r[:, :], bias[:, 0:1], bias[:, 3:4], ALU.add)
                nc.vector.tensor_tensor(bias_z[:, :], bias[:, 1:2], bias[:, 4:5], ALU.add).then_inc(s_bias, 1)
                dve.wait_ge(s_setup_used, 7)
                nc.vector.tensor_reduce(w_max[:, 0:1], vf[:, :, :], AX.XY, ALU.max, apply_absolute_value=True)
                chained(nc.vector.tensor_reduce(w_max[:, 1:2], wf[:, :], AX.X, ALU.max, apply_absolute_value=True))
                chained(nc.vector.tensor_tensor(w_max[:, 0:1], w_max[:, 0:1], w_max[:, 1:2], ALU.max))
                assert own[0] == OWN_MAX
                dve.wait_ge(s_pe_setup, 10)
                chained(nc.vector.tensor_reduce(top[:, 3:4], p_hn[0:1, 384:512], AX.X, ALU.max))
                chained(nc.vector.tensor_scalar(top[:, 3:4].bitcast(I32), top[:, 3:4].bitcast(I32), 0x7F800000, None,
                                                ALU.bitwise_and))
                chained(nc.vector.tensor_scalar(top[:, 3:4], top[:, 3:4], 2.0 ** -60, 2.0 ** 100, ALU.max, ALU.min))
                chained(nc.vector.reciprocal(top[:, 0:1], top[:, 3:4]))
                nc.vector.tensor_scalar(top[:, 2:3], top[:, 3:4], 1.0 / (S_V * S_AGG), None, ALU.mult)
                nc.vector.tensor_scalar(top[:, 1:2], top[:, 0:1], S_V * S_AGG / S_H, None, ALU.mult)
                chained(nc.vector.tensor_scalar(top[:, 0:1], top[:, 0:1], S_V, None, ALU.mult))
                assert own[0] == OWN_TOP
                dve.wait_ge(s_pe_setup, 11)
                chained(nc.vector.tensor_copy(scales[:, :], p_hn[:, 384:387]))
                assert own[0] == OWN_SCALES
                nc.vector.tensor_scalar(bias_hn[:, :], bias[:, 5:6], scales[:, 0:1], S_AGG, ALU.mult, ALU.mult
                                        ).then_inc(s_bias, 1)
                dve.wait_ge(s_setup_used, 8)
                nc.vector.scalar_tensor_tensor(VT[:, :, 1, :], vf[:, :, :], scales[:, 0:1], VT[:, :, 0, :],
                                               ALU.mult, ALU.subtract)
                nc.vector.scalar_tensor_tensor(WT[:, 1, :], wf[:, :], scales[:, 1:2], WT[:, 0, :],
                                               ALU.mult, ALU.subtract).then_inc(s_weights, 1)

            def step(s, k):
                if real(k - 1):
                    o, w = s - 1, (k - 1) % 2
                    wait(dve, s_pin, o + 1)
                    wait(dve, s_t, o + 1)
                    nc.vector.tensor_tensor(ru[w][:, :], ru[w][:, :], p_in[:, :], ALU.add).then_inc(s_u, 1)
                if first(k + 4):
                    q, w = s + 4, (k + 4) % 2
                    dve.wait_ge(s_x_in[w], 16 * (half(q) + 1))
                    for c in range(CH):
                        t = nc.vector.bn_stats(stats[w][:, c, :], xs[:, slot(q), c, :])
                    t.then_inc(s_stats_own, 1)
                if inner(k - 3):
                    o = s - 3
                    wait(dve, s_tr, o + 1)
                    nc.vector.tensor_copy(hN[:, slot(o), :, :, :], p_tr[:, :, :, :]).then_inc(s_hn, 1)
                if end(k - 2):
                    o = s - 2 - LAST
                    w = k % 2
                    wait(dve, s_ty, o + 1)
                    wait(dve, s_out[w], 16 * half(o))
                    j = slot(o) * CH
                    nc.vector.tensor_tensor(y[w].rearrange("p (c d) -> p c d", c=CH),
                                            p_x[:, :].rearrange("p (c d) -> p c d", c=CH),
                                            mask_t[:, bass.ds(j, CH)].unsqueeze(2).to_broadcast([128, CH, D]),
                                            ALU.mult).then_inc(s_ym, 1)
                if first(k + 3):
                    q, w = s + 3, (k + 3) % 2
                    dve.wait_ge(s_adj_in[w], 16 * (half(q) + 1))
                    if first(k + 4):
                        wait(dve, s_stats_own, q + 2)
                    nc.vector.tensor_scalar(A[:, slot(q), :, :], adj_in[w][:, :, :], 0.0, S_A,
                                            ALU.not_equal, ALU.mult).then_inc(s_a, 1)
                if first(k + 4):
                    q, w = s + 4, (k + 4) % 2
                    if k + 4 == 0:
                        wait(dve, s_stats_own, 1)
                    for c in range(CH):
                        t = nc.vector.bn_aggr(moments[w][:, c, :], stats[w][:, c, :])
                    t.then_inc(s_moments, 1)
                if real(k - 1):
                    o, w = s - 1, (k - 1) % 2
                    wait(dve, s_n, o + 1)
                    nc.vector.scalar_tensor_tensor(n[w][:, :], z[w][:, :], 1.0, n[w][:, :],
                                                   ALU.subtract, ALU.mult).then_inc(s_v, 1)
                    wait(dve, s_v, o + 1)
                    wait(dve, s_zh, o + 1)
                    if end(k - 1):
                        wait(dve, s_ty, o - LAST - 1)
                        target = h_end[w]
                    else:
                        target = h[:, slot(o), :]
                    nc.vector.scalar_tensor_tensor(target, n[w][:, :], -S_H, zh[w][:, :],
                                                   ALU.mult, ALU.add).then_inc(s_hnew, 1)
                if first(k + 4):
                    q, w = s + 4, (k + 4) % 2
                    wait(dve, s_rstd, q + 1)
                    wait(dve, s_tx, q - 1)
                    for c in range(CH):
                        t = nc.vector.tensor_scalar(xn[w][:, c, :], xs[:, slot(q), c, :], moments[w][:, c, 0:1],
                                                    rstd[w][:, c:c + 1], ALU.subtract, ALU.mult)
                    t.then_inc(s_xn, 1)
                if real(k + 1):
                    a, w = s + 1, (k + 1) % 2
                    wait(dve, s_agghi, a + 1)
                    nc.vector.tensor_tensor(agg[w][:, 1, :], p_agg[:, :], agg[w][:, 0, :], ALU.subtract
                                            ).then_inc(s_agglo, 1)
                if real(k):
                    if k == 0:
                        dve.wait_ge(s_bias, 2)
                    wait(dve, s_r, s + 1)
                    nc.vector.scalar_tensor_tensor(ru[k % 2][:, :], p_hn[:, :], bias_hn[:, :], ru[k % 2][:, :],
                                                   ALU.add, ALU.mult).then_inc(s_t, 1)

            setup()
            run(dve, step)

        @block.gpsimd
        def _(pool):
            nc.gpsimd.memset(minus_half[:, :], -0.5)
            nc.gpsimd.memset(eps[:, :], EPS).then_inc(s_pool_own, 1)
            nc.gpsimd.memset(ident[:, :], 0.0).then_inc(s_pool_own, 1)
            pool.wait_ge(s_pool_own, 2)
            nc.gpsimd.affine_select(out=ident[:, :], in_=ident[:, :], compare_op=ALU.not_equal, fill=1.0, base=0,
                                    pattern=[[-1, 128]], channel_multiplier=1).then_inc(s_ident, 1)
            pool.wait_ge(s_ident, 1)
            nc.gpsimd.tensor_copy(ident16[:, :], ident[:, :]).then_inc(s_ident, 1)

            def step(s, k):
                if first(k + 4):
                    q, w = s + 4, (k + 4) % 2
                    wait(pool, s_moments, q + 1)
                    nc.gpsimd.tensor_tensor(var_eps[w][:, :], moments[w][:, :, 1], eps[:, :], ALU.add
                                            ).then_inc(s_var, 1)
                    wait(pool, s_var, q + 1)
                    nc.gpsimd.tensor_tensor(rstd[w][:, :], var_eps[w][:, :], minus_half[:, :], ALU.pow
                                            ).then_inc(s_rstd, 1)
                if inner(k - 2):
                    o = s - 2
                    wait(pool, s_hi, o + 1)
                    nc.gpsimd.tensor_tensor(hT[:, slot(o), 1, :], h[:, slot(o), :], hT[:, slot(o), 0, :],
                                            ALU.subtract).then_inc(s_lo, 1)
                if first(k + 3):
                    q = s + 3
                    wait(pool, s_h0hi, q + 1)
                    nc.gpsimd.tensor_tensor(hT[:, slot(q), 1, :], h[:, slot(q), :], hT[:, slot(q), 0, :],
                                            ALU.subtract).then_inc(s_h0lo, 1)
                if end(k - 2):
                    o = s - 2 - LAST
                    w = k % 2
                    wait(pool, s_ym, o + 1)
                    nc.gpsimd.tensor_tensor(y[w], y[w], xs[:, slot(o), :, :].rearrange("p c d -> p (c d)"), ALU.add
                                            ).then_inc(s_y, 1)
                if real(k):
                    wait(pool, s_z, s + 1)
                    wait(pool, s_hnew, s - 1)
                    nc.gpsimd.tensor_tensor(zh[k % 2][:, :], z[k % 2][:, :], h[:, slot(s), :], ALU.mult
                                            ).then_inc(s_zh, 1)

            run(pool, step)


_INS = ["x", "adj", "nodemask", "L0_gnn_weight", "L0_gnn_w_ih", "L0_gnn_w_hh", "L0_gnn_b_ih", "L0_gnn_b_hh"]


def kernel(**inputs):
    import numpy as _np
    import concourse.bacc as _bacc
    from concourse import mybir as _mybir
    from concourse.bass_utils import run_bass_kernel_spmd as _run

    nc = _bacc.Bacc("TRN2", target_bir_lowering=False, num_devices=1)
    arrays, args = {}, []
    for name in _INS:
        a = _np.ascontiguousarray(inputs[name])
        arrays[f"in_{name}"] = a
        args.append(nc.dram_tensor(f"in_{name}", a.shape, _mybir.dt.from_np(a.dtype), kind="ExternalInput").ap())
    args.append(nc.dram_tensor("out_0", (B, N, D), FP32, kind="ExternalOutput").ap())
    gnn_program(nc, *args)
    return _run(nc, [arrays], core_ids=[0]).results[0]["out_0"]
```

```python
from contextlib import ExitStack

import concourse.bass as bass
from concourse import mybir

FP32 = mybir.dt.float32
FP16 = mybir.dt.float16
I32 = mybir.dt.int32
ALU = mybir.AluOpType
ACT = mybir.ActivationFunctionType
AX = mybir.AxisListType

B, N, D, L = 32, 256, 128, 5
G3 = 3 * D
PAIRS = B // 2
COLS = 2 * N
LOG_PAIRS = PAIRS.bit_length() - 1
CH = COLS // 128
STEPS = L * PAIRS
GP = 4
LOG_GP = GP.bit_length() - 1
GSTEPS = L * GP
GLAST = GSTEPS - GP
PREP = 4
STRETCHES = [(False, -PREP, 0)]
for _g in range(0, STEPS, GSTEPS):
    STRETCHES += [(False, _g, _g + GP), (True, _g + GP, _g + GLAST), (False, _g + GLAST, _g + GSTEPS)]
STRETCHES += [(False, STEPS, STEPS + 3)]
EPS = 1e-5

S_H = 256.0
S_A = 1.0 / 16.0
S_AGG = S_H * S_A
S_V = 2.0 ** 14


def gnn_program(nc, x, adj, nodemask, weight, w_ih, w_hh, b_ih, b_hh, out):
    x_v = x.rearrange("(t b) (k q) d -> t q (b k) d", b=2, q=128)
    adj_v = adj.rearrange("(t b) (k q) j -> t q (b k) j", b=2, q=128)
    out_v = out.rearrange("(t b) (k q) d -> t q (b k) d", b=2, q=128)
    mask_v = nodemask.rearrange("b (k q) -> (b k) q", q=128)

    ctx = ExitStack()
    with ctx:
        def sb(name, shape, dt):
            return ctx.enter_context(nc.sbuf_tensor(name, shape, dt))

        def pb(name, shape, dt=FP32):
            return ctx.enter_context(nc.psum_tensor(name, shape, dt))

        def sem(name):
            return ctx.enter_context(nc.semaphore(name))

        xs = sb("xs", [128, PAIRS, CH, D], FP32)
        h = sb("h", [128, PAIRS, COLS], FP32)
        hT = sb("hT", [128, PAIRS, 2, COLS], FP16)
        hN = sb("hN", [128, PAIRS, 2, CH, D], FP16)
        A = sb("A", [128, PAIRS, CH, N], FP16)
        VT = sb("VT", [128, L, 2, G3], FP16)
        WT = sb("WT", [128, 2, G3], FP16)
        ident = sb("ident", [128, 128], FP32)
        ones_row = sb("ones_row", [1, 128], FP32)
        minus_half = sb("minus_half", [128, CH], FP32)
        rows = sb("rows", [70, 128], FP32)
        mask_t = sb("mask_t", [128, 2 * B], FP32)
        bias = sb("bias", [128, 6], FP32)
        bias_r = sb("bias_r", [128, 1], FP32)
        bias_z = sb("bias_z", [128, 1], FP32)
        bias_hn = sb("bias_hn", [128, 1], FP32)
        w_max = sb("w_max", [128, 3], FP32)
        warm = sb("warm", [1, 1], FP32)
        top = sb("top", [1, 8], FP32)
        scales = sb("scales", [128, 3], FP32)
        adj_in = [sb(f"adj_in{i}", [128, CH, N], FP32) for i in range(2)]
        stats = [sb(f"stats{i}", [128, CH, 6], FP32) for i in range(2)]
        moments = [sb(f"moments{i}", [128, CH, 2], FP32) for i in range(2)]
        var_s = [sb(f"var_s{i}", [128, CH], FP32) for i in range(2)]
        minus_mean = [sb(f"minus_mean{i}", [128, CH], FP32) for i in range(2)]
        rstd = [sb(f"rstd{i}", [128, CH], FP32) for i in range(2)]
        shift = [sb(f"shift{i}", [128, CH], FP32) for i in range(2)]
        h0 = [sb(f"h0{i}", [128, CH, D], FP32) for i in range(2)]
        agg = [sb(f"agg{i}", [128, 2, COLS], FP16) for i in range(2)]
        ru = [sb(f"ru{i}", [128, COLS], FP32) for i in range(2)]
        z = [sb(f"z{i}", [128, COLS], FP32) for i in range(2)]
        n = [sb(f"n{i}", [128, COLS], FP32) for i in range(2)]
        zh = [sb(f"zh{i}", [128, COLS], FP32) for i in range(2)]
        raw = h[:, GP:PAIRS, :].rearrange("p a c -> p (a c)")
        w_raw = raw[:, 0:L * D].rearrange("p (l e) -> p l e", l=L)
        ih_raw = raw[:, 640:1024].rearrange("p (g e) -> p g e", g=3)
        hh_raw = raw[:, 1024:1408].rearrange("p (g e) -> p g e", g=3)
        ihT = raw[:, 1408:1792]
        wlT = raw[:, 1792:2432].rearrange("p (l d) -> p l d", l=L)
        y = [adj_in[1][:, 2 * i:2 * i + 2, :].rearrange("p a c -> p (a c)") for i in range(2)]

        p_r = pb("p_r", [128, COLS])
        p_z = pb("p_z", [128, COLS])
        p_in = pb("p_in", [128, COLS])
        p_hn = pb("p_hn", [128, COLS])
        p_agg = [pb(f"p_agg{i}", [128, COLS]) for i in range(2)]
        p_y = pb("p_y", [128, COLS])
        p_s = pb("p_s", [128, COLS])

        s_small_in = sem("small_in")
        s_w_in = [sem(f"w_in{i}") for i in range(3)]
        s_x_in = [sem(f"x_in{i}") for i in range(2)]
        s_adj_in = sem("adj_in_sem")
        s_out = [sem(f"out_sent{i}") for i in range(2)]
        s_pool_own = sem("pool_own")
        s_ident = sem("ident_ready")
        s_ones = sem("ones_ready")
        s_dve_own = sem("dve_own")
        s_pe_setup = sem("pe_setup")
        s_setup_used = sem("setup_used")
        s_whi = sem("weights_hi")
        s_weights = sem("weights_ready")
        s_scales = sem("scales_ready")
        s_bias = sem("bias_ready")
        s_stats_own = sem("stats_own")
        s_moments = sem("moments_ready")
        s_var = sem("var_ready")
        s_rstd = sem("rstd_ready")
        s_shift = sem("shift_ready")
        s_x0 = sem("h0_ready")
        s_h0hi = sem("h0_hi_ready")
        s_h0lo = sem("h0_lo_ready")
        s_ht0 = sem("hT0_ready")
        s_h0 = sem("h0_in_h")
        s_a = sem("a_ready")
        s_agg = sem("agg_done")
        s_agghi = sem("agg_hi_ready")
        s_agglo = sem("agg_lo_ready")
        s_pr = sem("p_r_done")
        s_pz = sem("p_z_done")
        s_pin = sem("p_in_done")
        s_r = sem("r_ready")
        s_z = sem("z_ready")
        s_t = sem("t_ready")
        s_u = sem("u_ready")
        s_n = sem("n_ready")
        s_v = sem("v_own")
        s_zh = sem("zh_ready")
        s_hnew = sem("h_new_ready")
        s_hi = sem("hi_ready")
        s_lo = sem("lo_ready")
        s_hn = [sem(f"hN_ready{i}") for i in range(2)]
        s_ty = sem("ty_done")
        s_ysum = sem("y_summed")
        s_ym = sem("y_masked")
        s_y = sem("y_ready")

        block = ctx.enter_context(nc.Block())

        OWN_MAX, OWN_TOP = 1, 8

        def wait(eng, s, count):
            if isinstance(count, int) and count <= 0:
                return
            eng.wait_ge(s, count)

        def group(k):
            return k // GSTEPS

        def slot(s, k):
            return (s & (GP - 1)) + GP * group(k)

        def half(s):
            return s >> 1

        def real(k):
            return 0 <= k < STEPS

        def split(k):
            return real(k) and k < STEPS - 1

        def end(k):
            return real(k) and k % GSTEPS >= GLAST

        def end_count(s, k):
            return s - GLAST * (group(k) + 1)

        def first(k):
            return real(k) and k % GSTEPS < GP

        def prepared(s, k, stage):
            if -PREP + stage <= k < GP - PREP + stage:
                return s + PREP - stage, (k + PREP - stage) % 2
            start = GSTEPS * group(k) + GP
            if k >= 0 and start <= k < STEPS - GSTEPS and k % GP == stage:
                return ((s - start) >> LOG_GP) + GP * (group(k) + 1), 0
            return None

        def before(q):
            return q - 1 if isinstance(q, int) and q < GP else q

        def run(eng, step):
            for loop, a, b in STRETCHES:
                if loop:
                    with eng.Fori(a // GP, b // GP) as i:
                        for k in range(GP):
                            step(i * GP + k, a + k)
                else:
                    for s in range(a, b):
                        step(s, s)

        @block.sync
        def _(sp):
            def pair_of(q):
                return nc.s_assert_within(q, 0, PAIRS - 1, skip_runtime_bounds_check_because="the loops end there")

            def slot_of(s, k):
                if isinstance(s, int):
                    return slot(s, k)
                return pair_of(s - (s >> LOG_GP) * GP + GP * group(k))

            def to_nodes(pair):
                return sp.dma_start_transpose(hN[:, pair, :, :, :].rearrange("p t c d -> p (t c) d"),
                                              hT[:, pair, :, :].rearrange("p t c -> p (t c)"))

            def to_features(pair):
                return sp.dma_start_transpose(hT[:, pair, :, :].rearrange("p t (c q) -> p (t c) q", c=CH),
                                              hN[:, pair, :, :, :].rearrange("p t c d -> p (t c d)"))

            def load_adj(q, w):
                wait(sp, s_adj_in, 16 * q)
                wait(sp, s_a, before(q))
                sp.dma_start(adj_in[w][:, :, :], adj_v[pair_of(q)]).then_inc(s_adj_in, 16)

            def load_x(q):
                wait(sp, s_x_in[1], 16 * (q - 2))
                sp.dma_start(xs[:, pair_of(q), :, :], x_v[pair_of(q)]).then_inc(s_x_in[1], 16)

            def first_parts(s, k):
                if p := prepared(s, k, 2):
                    q, _ = p
                    wait(sp, s_h0lo, q + 1)
                    wait(sp, s_ht0, 16 * q)
                    to_features(pair_of(q)).then_inc(s_ht0, 16)

            def step(s, k):
                if k >= 0 and (p := prepared(s, k, 0)):
                    load_adj(*p)
                    if GP <= k < STEPS - GSTEPS - GP:
                        load_x(p[0] + 1)
                first_parts(s, k)
                if split(k - 1):
                    o, w = s - 1, (k - 1) % 2
                    wait(sp, s_lo, o + 1)
                    wait(sp, s_hn[w], 16 * half(o))
                    to_nodes(slot_of(o, k - 1)).then_inc(s_hn[w], 16)
                if -PREP + 1 < k < 0 and (p := prepared(s, k, 0)):
                    load_adj(*p)
                if k == 0:
                    load_x(GP)
                if end(k - 3):
                    o, w = s - 3, (k - 3) % 2
                    e = end_count(o, k - 3)
                    wait(sp, s_y, e + 1)
                    sp.dma_start(out_v[slot_of(o, k - 3)], y[w].rearrange("p (c d) -> p c d", c=CH)
                                 ).then_inc(s_out[w], 16)

            sp.dma_start(xs[:, 0, :, :], x_v[0]).then_inc(s_x_in[0], 16)
            sp.dma_start(w_raw, weight.rearrange("l d e -> d l e")).then_inc(s_w_in[2], 16)
            sp.dma_start(xs[:, 1, :, :], x_v[1]).then_inc(s_x_in[1], 16)
            load_adj(0, 0)
            sp.wait_ge(s_x_in[1], 16)
            sp.dma_start(xs[:, 2:GP, :, :].rearrange("q t c d -> q (t c) d"),
                         x_v[2:GP].rearrange("t q c d -> q (t c) d")).then_inc(s_x_in[1], 16)
            load_adj(1, 1)
            run(sp, step)
            for w in range(2):
                sp.wait_ge(s_out[w], 16 * (PAIRS // 2))

        @block.tensor
        def _(pe):
            def setup(k):
                if k == -PREP:
                    pe.wait_ge(s_ident, 1)
                    pe.wait_ge(s_w_in[0], 16)
                    for g in range(3):
                        t = nc.tensor.transpose(p_r[:, g * D:(g + 1) * D], ih_raw[:, g, :], ident[:, :])
                    t.then_inc(s_pe_setup, 1)
                    pe.wait_ge(s_w_in[2], 16)
                    for l in range(L):
                        bank = p_z if l < 4 else p_in
                        c = (l % 4) * D
                        t = nc.tensor.transpose(bank[:, c:c + D], w_raw[:, l, :], ident[:, :])
                    t.then_inc(s_pe_setup, 1)
                    pe.wait_ge(s_w_in[1], 16)
                    for g in range(3):
                        nc.tensor.transpose(p_hn[:, g * D:(g + 1) * D], hh_raw[:, g, :], ident[:, :])
                if k == -PREP + 1:
                    pe.wait_ge(s_dve_own, OWN_MAX)
                    for i in range(3):
                        t = nc.tensor.transpose(p_s[0:1, i * 128:(i + 1) * 128], w_max[:, i:i + 1], ident[:, :])
                    t.then_inc(s_pe_setup, 1)
                    pe.wait_ge(s_setup_used, 1)
                    for l, bank in ((0, p_agg[1]), (1, p_in)):
                        nc.tensor.matmul(bank[:, 0:G3], wlT[:, l, :], ihT[:, :], start=True, stop=True
                                         ).then_inc(s_pe_setup, 1)
                    pe.wait_ge(s_ones, 1)
                    pe.wait_ge(s_dve_own, OWN_TOP)
                    nc.tensor.matmul(p_s[:, 384:387], ones_row[0:1, :], top[0:1, 0:3], start=True, stop=True
                                     ).then_inc(s_pe_setup, 1)
                if k == -PREP + 2:
                    pe.wait_ge(s_small_in, 48)
                    pe.wait_ge(s_scales, 1)
                    nc.tensor.transpose(p_s[:, 0:70], rows[:, :], ident[0:70, 0:70]
                                        ).then_inc(s_pe_setup, 1)
                if 0 <= k < L - 2:
                    l = k + 2
                    wait(pe, s_weights, l)
                    wait(pe, s_bias, 1)
                    nc.tensor.matmul(p_s[:, 0:G3], wlT[:, l, :], ihT[:, :], start=True, stop=True
                                     ).then_inc(s_pe_setup, 1)

            def aggregate(s, k):
                if not real(k + 1):
                    return
                a, w = s + 1, (k + 1) % 2
                pair = slot(a, k + 1)
                if first(k + 1):
                    wait(pe, s_h0lo, pair + 1)
                    wait(pe, s_a, pair + 1)
                    if k + 1 == 1:
                        pe.wait_ge(s_weights, 1)
                else:
                    wait(pe, s_hn[w], 16 * (half(a - GP) + 1))
                wait(pe, s_agglo, a - 1)
                for b in range(2):
                    for m in range(4):
                        hf, part = m // 2, m % 2
                        t = nc.tensor.matmul(p_agg[w][:, b * N:(b + 1) * N], hN[:, pair, part, 2 * b + hf, :],
                                             A[:, pair, 2 * b + hf, :], start=(m == 0), stop=(m == 3))
                t.then_inc(s_agg, 1)

            def step(s, k):
                if k < 0:
                    setup(k)
                if k == STEPS + 1:
                    o = STEPS - 1
                    wait(pe, s_hnew, o + 1)
                    for c in range(CH):
                        t = nc.tensor.transpose(p_y[:, c * 128:(c + 1) * 128],
                                                h[:, slot(o, o), c * 128:(c + 1) * 128], ident[:, :])
                    t.then_inc(s_ty, 1)
                if k < 0:
                    aggregate(s, k)
                if real(k):
                    layer = (s - GSTEPS * group(k)) >> LOG_GP
                    pair = slot(s, k)
                    hi, lo = hT[:, pair, 0, :], hT[:, pair, 1, :]
                    ahi, alo = agg[k % 2][:, 0, :], agg[k % 2][:, 1, :]

                    def products(bank, gate, table, data, start, stop):
                        c = gate * D
                        nc.tensor.matmul(bank[:, :], table[:, 0, c:c + D], data[0], start=start, stop=False)
                        nc.tensor.matmul(bank[:, :], table[:, 0, c:c + D], data[1], start=False, stop=False)
                        return nc.tensor.matmul(bank[:, :], table[:, 1, c:c + D], data[0], start=False, stop=stop)

                    V = VT[:, layer, :, :]
                    if k == 0:
                        pe.wait_ge(s_weights, 1)
                    if k == GP:
                        pe.wait_ge(s_weights, L)
                    if first(k):
                        wait(pe, s_ht0, 16 * (pair + 1))
                    wait(pe, s_t, s)
                    products(p_hn, 2, WT, (hi, lo), True, True)
                    wait(pe, s_r, s)
                    products(p_r, 0, WT, (hi, lo), True, False)
                    wait(pe, s_agglo, s + 1)
                    products(p_r, 0, V, (ahi, alo), False, True).then_inc(s_pr, 1)
                    aggregate(s, k)
                    wait(pe, s_z, s)
                    products(p_z, 1, WT, (hi, lo), True, False)
                    products(p_z, 1, V, (ahi, alo), False, True).then_inc(s_pz, 1)
                    setup(k)
                    if k == 0:
                        pe.wait_ge(s_weights, 2)
                    wait(pe, s_u, s)
                    products(p_in, 2, V, (ahi, alo), True, True).then_inc(s_pin, 1)

            run(pe, step)

        @block.scalar
        def _(act):
            def setup(k):
                if k == -PREP:
                    act.dma_start(ih_raw, w_ih.rearrange("(g f) e -> f g e", g=3)).then_inc(s_w_in[0], 16)
                    act.dma_start(hh_raw, w_hh.rearrange("(g f) e -> f g e", g=3)).then_inc(s_w_in[1], 16)
                    act.wait_ge(s_ones, 1)
                    nc.scalar.activation(warm[:, :], ones_row[0:1, 0:1], ACT.Sigmoid)
                    act.dma_start(rows[0:64, :], mask_v).then_inc(s_small_in, 16)
                    act.dma_start(rows[64:67, :], b_ih.rearrange("(g f) -> g f", g=3)).then_inc(s_small_in, 16)
                    act.dma_start(rows[67:70, :], b_hh.rearrange("(g f) -> g f", g=3)).then_inc(s_small_in, 16)
                    act.wait_ge(s_pe_setup, 1)
                    nc.scalar.activation(ihT[:, :], p_r[:, 0:G3], ACT.Copy)
                    act.wait_ge(s_pe_setup, 2)
                    nc.scalar.activation(wlT[:, 0:4, :].rearrange("p l d -> p (l d)"), p_z[:, :], ACT.Copy)
                    nc.scalar.activation(wlT[:, 4, :], p_in[:, 0:D], ACT.Copy).then_inc(s_setup_used, 1)
                if k == -PREP + 3:
                    act.wait_ge(s_scales, 1)
                    nc.scalar.activation(WT[:, 0, :], p_hn[:, 0:G3], ACT.Copy, scale=scales[:, 1:2])
                    act.wait_ge(s_pe_setup, 4)
                    nc.scalar.activation(VT[:, 0, 0, :], p_agg[1][:, 0:G3], ACT.Copy, scale=scales[:, 0:1]
                                         ).then_inc(s_whi, 1)
                if 0 <= k < L - 2:
                    l = k + 2
                    act.wait_ge(s_pe_setup, 6 + l)
                    nc.scalar.activation(VT[:, l, 0, :], p_s[:, 0:G3], ACT.Copy, scale=scales[:, 0:1]
                                         ).then_inc(s_whi, 1)

            def first_state(s, k, part):
                if p := prepared(s, k, 0 if part == 0 and k >= GP else 1):
                    q, w = p
                    if part == 0:
                        wait(act, s_shift, q + 1)
                        wait(act, s_h0lo, before(q))
                    for c in range(2 * part, 2 * part + 2):
                        t = nc.scalar.activation(h0[w][:, c, :], xs[:, q, c, :], ACT.Relu,
                                                 bias=shift[w][:, c:c + 1], scale=rstd[w][:, c:c + 1])
                    if part == 1:
                        t.then_inc(s_x0, 1)

            def step(s, k):
                if k < 0:
                    setup(k)
                if real(k - 1):
                    o = s - 1
                    wait(act, s_u, o + 1)
                    nc.scalar.activation(n[(k - 1) % 2][:, :], ru[(k - 1) % 2][:, :], ACT.Tanh,
                                         bias=bias[:, 2:3], scale=scales[:, 2:3]).then_inc(s_n, 1)
                if p := prepared(s, k, 2):
                    q, w = p
                    wait(act, s_x0, q + 1)
                    nc.scalar.activation(hN[:, q, 0, :, :], h0[w][:, :, :], ACT.Copy).then_inc(s_h0hi, 1)
                if real(k):
                    if k == 0:
                        act.wait_ge(s_bias, 1)
                    wait(act, s_pr, s + 1)
                    wait(act, s_n, s - 1)
                    nc.scalar.activation(ru[k % 2][:, :], p_r[:, :], ACT.Sigmoid, bias=bias_r[:, :],
                                         scale=scales[:, 2:3]).then_inc(s_r, 1)
                if real(k + 1):
                    a, w = s + 1, (k + 1) % 2
                    wait(act, s_agg, a + 1)
                    wait(act, s_pin, a - 1)
                    nc.scalar.activation(agg[w][:, 0, :], p_agg[w][:, :], ACT.Copy).then_inc(s_agghi, 1)
                if k == -PREP + 3:
                    act.wait_ge(s_pe_setup, 5)
                    nc.scalar.activation(VT[:, 1, 0, :], p_in[:, 0:G3], ACT.Copy, scale=scales[:, 0:1]
                                         ).then_inc(s_whi, 1)
                if split(k - 1):
                    o = s - 1
                    pair = slot(o, k - 1)
                    wait(act, s_hnew, o + 1)
                    nc.scalar.activation(hT[:, pair, 0, :], h[:, pair, :], ACT.Copy).then_inc(s_hi, 1)
                if real(k):
                    wait(act, s_pz, s + 1)
                    wait(act, s_hnew, s - 1)
                    nc.scalar.activation(z[k % 2][:, :], p_z[:, :], ACT.Sigmoid, bias=bias_z[:, :],
                                         scale=scales[:, 2:3]).then_inc(s_z, 1)
                if k >= 0:
                    setup(k)
                first_state(s, k, 0)
                first_state(s, k, 1)

            run(act, step)

        @block.vector
        def _(dve):
            own = [0]

            def chained(ins):
                own[0] += 1
                ins.then_inc(s_dve_own, 1)
                dve.wait_ge(s_dve_own, own[0])

            def setup(k):
                if k == -PREP:
                    dve.wait_ge(s_w_in[0], 16)
                    nc.vector.tensor_reduce(w_max[:, 0:1], ih_raw, AX.XY, ALU.max, apply_absolute_value=True)
                    dve.wait_ge(s_w_in[2], 16)
                    nc.vector.tensor_reduce(w_max[:, 1:2], w_raw, AX.XY, ALU.max, apply_absolute_value=True)
                    dve.wait_ge(s_w_in[1], 16)
                    chained(nc.vector.tensor_reduce(w_max[:, 2:3], hh_raw, AX.XY, ALU.max, apply_absolute_value=True))
                    assert own[0] == OWN_MAX
                if k == -PREP + 1:
                    dve.wait_ge(s_pe_setup, 3)
                    chained(nc.vector.tensor_reduce(top[:, 4:7], p_s[0:1, 0:384].rearrange("p (i c) -> p i c", i=3),
                                                    AX.X, ALU.max))
                    chained(nc.vector.tensor_scalar(top[:, 4:5], top[:, 4:5], float(D), top[:, 5:6],
                                                    ALU.mult, ALU.mult))
                    chained(nc.vector.tensor_tensor(top[:, 3:4], top[:, 4:5], top[:, 6:7], ALU.max))
                    chained(nc.vector.tensor_scalar(top[:, 3:4].bitcast(I32), top[:, 3:4].bitcast(I32), 0x7F800000,
                                                    None, ALU.bitwise_and))
                    chained(nc.vector.tensor_scalar(top[:, 3:4], top[:, 3:4], 2.0 ** -60, 2.0 ** 100,
                                                    ALU.max, ALU.min))
                    chained(nc.vector.reciprocal(top[:, 7:8], top[:, 3:4]))
                    nc.vector.tensor_scalar(top[:, 2:3], top[:, 3:4], 1.0 / (S_V * S_AGG), None, ALU.mult)
                    nc.vector.tensor_scalar(top[:, 1:2], top[:, 7:8], S_V * S_AGG / S_H, None, ALU.mult)
                    chained(nc.vector.tensor_scalar(top[:, 0:1], top[:, 7:8], S_V, None, ALU.mult))
                    assert own[0] == OWN_TOP
                if k == 0:
                    dve.wait_ge(s_whi, 2)
                    nc.vector.scalar_tensor_tensor(VT[:, 1, 1, :], p_in[:, 0:G3], scales[:, 0:1], VT[:, 1, 0, :],
                                                   ALU.mult, ALU.subtract).then_inc(s_weights, 1)
                    dve.wait_ge(s_pe_setup, 7)
                    nc.vector.tensor_scalar(mask_t[:, :], p_s[:, 0:64], 1.0 / S_H, None, ALU.mult)
                    chained(nc.vector.tensor_copy(bias[:, :], p_s[:, 64:70]))
                    nc.vector.tensor_tensor(bias_r[:, :], bias[:, 0:1], bias[:, 3:4], ALU.add)
                    nc.vector.tensor_tensor(bias_z[:, :], bias[:, 1:2], bias[:, 4:5], ALU.add)
                    nc.vector.tensor_scalar(bias_hn[:, :], bias[:, 5:6], scales[:, 0:1], S_AGG, ALU.mult, ALU.mult
                                            ).then_inc(s_bias, 1)
                if 1 <= k < L - 1:
                    l = k + 1
                    dve.wait_ge(s_whi, 1 + l)
                    nc.vector.scalar_tensor_tensor(VT[:, l, 1, :], p_s[:, 0:G3], scales[:, 0:1], VT[:, l, 0, :],
                                                   ALU.mult, ALU.subtract).then_inc(s_weights, 1)

            def result_parts(s, k):
                if end(k - 3) and split(k - 3):
                    o, w = s - 3, (k - 3) % 2
                    e = end_count(o, k - 3)
                    wait(dve, s_hn[w], 16 * (half(o) + 1))
                    wait(dve, s_out[w], 16 * half(e))
                    parts = hN[:, slot(o, k - 3), :, :, :].rearrange("p t c d -> p t (c d)")
                    nc.vector.tensor_tensor(y[w], parts[:, 0, :], parts[:, 1, :], ALU.add).then_inc(s_ysum, 1)

            def masked(s, k):
                if not end(k - 3):
                    return
                o, w = s - 3, (k - 3) % 2
                e = end_count(o, k - 3)
                if split(k - 3):
                    result = y[w]
                    wait(dve, s_ysum, e + 1)
                else:
                    result = p_y[:, :]
                    wait(dve, s_ty, 1)
                    wait(dve, s_out[w], 16 * half(e))
                nc.vector.tensor_tensor(y[w].rearrange("p (c d) -> p c d", c=CH),
                                        result.rearrange("p (c d) -> p c d", c=CH),
                                        mask_t[:, bass.ds(slot(o, k - 3) * CH, CH)].unsqueeze(2)
                                        .to_broadcast([128, CH, D]), ALU.mult).then_inc(s_ym, 1)

            def moments_of(s, k):
                if p := prepared(s, k, 0):
                    q, w = p
                    for c in range(CH):
                        t = nc.vector.bn_aggr(moments[w][:, c, :], stats[w][:, c, :])
                    t.then_inc(s_moments, 1)
                    wait(dve, s_moments, q + 1)
                    wait(dve, s_shift, before(q))
                    nc.vector.tensor_scalar(var_s[w][:, :], moments[w][:, :, 1], EPS, 1.0 / S_H ** 2,
                                            ALU.add, ALU.mult)
                    nc.vector.tensor_scalar(minus_mean[w][:, :], moments[w][:, :, 0], -1.0, None, ALU.mult
                                            ).then_inc(s_var, 1)

            def adjacency_tile(s, k):
                if p := prepared(s, k, 1 if k < GP else 2):
                    q, w = p
                    wait(dve, s_adj_in, 16 * (q + 1))
                    nc.vector.tensor_scalar(A[:, q, :, :], adj_in[w][:, :, :], 0.0, S_A,
                                            ALU.not_equal, ALU.mult).then_inc(s_a, 1)

            def step(s, k):
                if real(k - 1):
                    o, w = s - 1, (k - 1) % 2
                    wait(dve, s_pin, o + 1)
                    wait(dve, s_t, o + 1)
                    nc.vector.tensor_tensor(ru[w][:, :], ru[w][:, :], p_in[:, :], ALU.add).then_inc(s_u, 1)
                if k == -PREP + 3:
                    dve.wait_ge(s_whi, 1)
                    nc.vector.scalar_tensor_tensor(WT[:, 1, :], p_hn[:, 0:G3], scales[:, 1:2], WT[:, 0, :],
                                                   ALU.mult, ALU.subtract)
                    nc.vector.scalar_tensor_tensor(VT[:, 0, 1, :], p_agg[1][:, 0:G3], scales[:, 0:1], VT[:, 0, 0, :],
                                                   ALU.mult, ALU.subtract).then_inc(s_weights, 1)
                if p := prepared(s, k, 0):
                    q, w = p
                    if k == -PREP:
                        dve.wait_ge(s_x_in[0], 16)
                    else:
                        wait(dve, s_x_in[1], 16 * min(q, 2) if k <= 0 else 16 * (q - 1))
                    for c in range(CH):
                        t = nc.vector.bn_stats(stats[w][:, c, :], xs[:, q, c, :])
                    t.then_inc(s_stats_own, 1)
                    wait(dve, s_stats_own, q + 1)
                if k < 0:
                    moments_of(s, k)
                if k > 0:
                    setup(k)
                result_parts(s, k)
                if real(k - 1):
                    o, w = s - 1, (k - 1) % 2
                    wait(dve, s_n, o + 1)
                    nc.vector.scalar_tensor_tensor(n[w][:, :], z[w][:, :], 1.0, n[w][:, :],
                                                   ALU.subtract, ALU.mult).then_inc(s_v, 1)
                if k >= 0:
                    moments_of(s, k)
                masked(s, k)
                if k <= 0:
                    setup(k)
                if k < 0:
                    adjacency_tile(s, k)
                if k == -PREP + 1:
                    dve.wait_ge(s_pe_setup, 6)
                    nc.vector.tensor_copy(scales[:, :], p_s[:, 384:387]).then_inc(s_scales, 1)
                if real(k - 1):
                    o, w = s - 1, (k - 1) % 2
                    wait(dve, s_v, o + 1)
                    wait(dve, s_zh, o + 1)
                    nc.vector.scalar_tensor_tensor(h[:, slot(o, k - 1), :], n[w][:, :], -S_H, zh[w][:, :],
                                                   ALU.mult, ALU.add).then_inc(s_hnew, 1)
                if real(k):
                    wait(dve, s_r, s + 1)
                    nc.vector.scalar_tensor_tensor(ru[k % 2][:, :], p_hn[:, :], bias_hn[:, :], ru[k % 2][:, :],
                                                   ALU.add, ALU.mult).then_inc(s_t, 1)
                if real(k + 1):
                    a, w = s + 1, (k + 1) % 2
                    wait(dve, s_agghi, a + 1)
                    nc.vector.tensor_tensor(agg[w][:, 1, :], p_agg[w][:, :], agg[w][:, 0, :], ALU.subtract
                                            ).then_inc(s_agglo, 1)
                if k >= 0:
                    adjacency_tile(s, k)
                if p := prepared(s, k, 3):
                    q, _ = p
                    wait(dve, s_ht0, 16 * (q + 1))
                    nc.vector.tensor_tensor(h[:, q, :], hT[:, q, 0, :], hT[:, q, 1, :], ALU.add).then_inc(s_h0, 1)

            nc.vector.memset(ones_row[:, :], 1.0).then_inc(s_ones, 1)
            run(dve, step)

        @block.gpsimd
        def _(pool):
            nc.gpsimd.memset(minus_half[:, :], -0.5)
            nc.gpsimd.memset(ident[:, :], 0.0).then_inc(s_pool_own, 1)
            pool.wait_ge(s_pool_own, 1)
            nc.gpsimd.affine_select(out=ident[:, :], in_=ident[:, :], compare_op=ALU.not_equal, fill=1.0, base=0,
                                    pattern=[[-1, 128]], channel_multiplier=1).then_inc(s_ident, 1)

            def step(s, k):
                if p := prepared(s, k, 2):
                    q, w = p
                    wait(pool, s_h0hi, q + 1)
                    nc.gpsimd.tensor_tensor(hN[:, q, 1, :, :], h0[w][:, :, :], hN[:, q, 0, :, :], ALU.subtract
                                            ).then_inc(s_h0lo, 1)
                if p := prepared(s, k, 0):
                    q, w = p
                    wait(pool, s_var, q + 1)
                    wait(pool, s_x0, before(q))
                    nc.gpsimd.tensor_tensor(rstd[w][:, :], var_s[w][:, :], minus_half[:, :], ALU.pow
                                            ).then_inc(s_rstd, 1)
                    wait(pool, s_rstd, q + 1)
                    nc.gpsimd.tensor_tensor(shift[w][:, :], minus_mean[w][:, :], rstd[w][:, :], ALU.mult
                                            ).then_inc(s_shift, 1)
                if end(k - 3):
                    o, w = s - 3, (k - 3) % 2
                    wait(pool, s_ym, end_count(o, k - 3) + 1)
                    nc.gpsimd.tensor_tensor(y[w], y[w], xs[:, slot(o, k - 3), :, :].rearrange("p c d -> p (c d)"),
                                            ALU.add).then_inc(s_y, 1)
                if split(k - 1):
                    o = s - 1
                    pair = slot(o, k - 1)
                    wait(pool, s_hi, o + 1)
                    nc.gpsimd.tensor_tensor(hT[:, pair, 1, :], h[:, pair, :], hT[:, pair, 0, :], ALU.subtract
                                            ).then_inc(s_lo, 1)
                if real(k):
                    if first(k):
                        wait(pool, s_h0, slot(s, k) + 1)
                    wait(pool, s_z, s + 1)
                    wait(pool, s_hnew, s - 1)
                    nc.gpsimd.tensor_tensor(zh[k % 2][:, :], z[k % 2][:, :], h[:, slot(s, k), :], ALU.mult
                                            ).then_inc(s_zh, 1)
            run(pool, step)


_INS = ["x", "adj", "nodemask", "L0_gnn_weight", "L0_gnn_w_ih", "L0_gnn_w_hh", "L0_gnn_b_ih", "L0_gnn_b_hh"]


def kernel(**inputs):
    import numpy as _np
    import concourse.bacc as _bacc
    from concourse import mybir as _mybir
    from concourse.bass_utils import run_bass_kernel_spmd as _run

    nc = _bacc.Bacc("TRN2", target_bir_lowering=False, num_devices=1)
    arrays, args = {}, []
    for name in _INS:
        a = _np.ascontiguousarray(inputs[name])
        arrays[f"in_{name}"] = a
        args.append(nc.dram_tensor(f"in_{name}", a.shape, _mybir.dt.from_np(a.dtype), kind="ExternalInput").ap())
    args.append(nc.dram_tensor("out_0", (B, N, D), FP32, kind="ExternalOutput").ap())
    gnn_program(nc, *args)
    return _run(nc, [arrays], core_ids=[0]).results[0]["out_0"]
```

```python
from contextlib import ExitStack

import concourse.bass as bass
from concourse import mybir

FP32 = mybir.dt.float32
FP16 = mybir.dt.float16
I32 = mybir.dt.int32
ALU = mybir.AluOpType
ACT = mybir.ActivationFunctionType
AX = mybir.AxisListType

B, N, D, L = 32, 256, 128, 5
G3 = 3 * D
PAIRS = B // 2
COLS = 2 * N
CH = COLS // 128
STEPS = L * PAIRS
GP = 4
LOG_GP = GP.bit_length() - 1
GSTEPS = L * GP
GLAST = GSTEPS - GP
PREP = 4
STRETCHES = [(False, -PREP, 0)]
for _g in range(0, STEPS, GSTEPS):
    STRETCHES += [(False, _g, _g + GP), (True, _g + GP, _g + GLAST), (False, _g + GLAST, _g + GSTEPS)]
STRETCHES += [(False, STEPS, STEPS + 3)]
DIRECT = 3
LAST = [(STEPS - 3, 0, CH), (STEPS - 2, 0, CH), (STEPS - 1, 0, CH // 2), (STEPS - 1, CH // 2, CH)]
EPS = 1e-5

S_H = 256.0
S_A = 1.0 / 16.0
S_AGG = S_H * S_A
S_V = 2.0 ** 14


def gnn_program(nc, x, adj, nodemask, weight, w_ih, w_hh, b_ih, b_hh, out):
    x_v = x.rearrange("(t b) (k q) d -> t q (b k) d", b=2, q=128)
    adj_v = adj.rearrange("(t b) (k q) j -> t q (b k) j", b=2, q=128)
    out_v = out.rearrange("(t b) (k q) d -> t q (b k) d", b=2, q=128)
    mask_v = nodemask.rearrange("b (k q) -> (b k) q", q=128)

    ctx = ExitStack()
    with ctx:
        def sb(name, shape, dt):
            return ctx.enter_context(nc.sbuf_tensor(name, shape, dt))

        def pb(name, shape, dt=FP32):
            return ctx.enter_context(nc.psum_tensor(name, shape, dt))

        def sem(name):
            return ctx.enter_context(nc.semaphore(name))

        xs = sb("xs", [128, PAIRS, CH, D], FP32)
        h = sb("h", [128, PAIRS, COLS], FP32)
        hT = sb("hT", [128, PAIRS, 2, COLS], FP16)
        hN = sb("hN", [128, PAIRS, 2, CH, D], FP16)
        A = sb("A", [128, PAIRS, CH, N], FP16)
        VT = sb("VT", [128, L, 2, G3], FP16)
        WT = sb("WT", [128, 2, G3], FP16)
        ident = sb("ident", [128, 128], FP32)
        ones_row = sb("ones_row", [1, 128], FP32)
        minus_half = sb("minus_half", [128, CH], FP32)
        rows = sb("rows", [70, 128], FP32)
        mask_t = sb("mask_t", [128, 2 * B], FP32)
        bias = sb("bias", [128, 6], FP32)
        bias_r = sb("bias_r", [128, 1], FP32)
        bias_z = sb("bias_z", [128, 1], FP32)
        bias_hn = sb("bias_hn", [128, 1], FP32)
        w_max = sb("w_max", [128, 3], FP32)
        warm = sb("warm", [1, 1], FP32)
        top = sb("top", [1, 8], FP32)
        scales = sb("scales", [128, 3], FP32)
        adj_in = [sb(f"adj_in{i}", [128, CH, N], FP32) for i in range(2)]
        stats = [sb(f"stats{i}", [128, CH, 6], FP32) for i in range(2)]
        moments = [sb(f"moments{i}", [128, CH, 2], FP32) for i in range(2)]
        var_s = [sb(f"var_s{i}", [128, CH], FP32) for i in range(2)]
        minus_mean = [sb(f"minus_mean{i}", [128, CH], FP32) for i in range(2)]
        rstd = [sb(f"rstd{i}", [128, CH], FP32) for i in range(2)]
        shift = [sb(f"shift{i}", [128, CH], FP32) for i in range(2)]
        h0 = [sb(f"h0{i}", [128, CH, D], FP32) for i in range(2)]
        agg = [sb(f"agg{i}", [128, 2, COLS], FP16) for i in range(2)]
        ru = [sb(f"ru{i}", [128, COLS], FP32) for i in range(2)]
        z = [sb(f"z{i}", [128, COLS], FP32) for i in range(2)]
        n = [sb(f"n{i}", [128, COLS], FP32) for i in range(2)]
        zh = [sb(f"zh{i}", [128, COLS], FP32) for i in range(2)]
        raw = h[:, GP:PAIRS, :].rearrange("p a c -> p (a c)")
        w_raw = raw[:, 0:L * D].rearrange("p (l e) -> p l e", l=L)
        ih_raw = raw[:, 640:1024].rearrange("p (g e) -> p g e", g=3)
        hh_raw = raw[:, 1024:1408].rearrange("p (g e) -> p g e", g=3)
        ihT = raw[:, 1408:1792]
        wlT = raw[:, 1792:2432].rearrange("p (l d) -> p l d", l=L)
        y = [adj_in[1][:, 2 * i:2 * i + 2, :].rearrange("p a c -> p (a c)") for i in range(2)]
        y_last = [adj_in[0][:, 0:2, :].rearrange("p a (c d) -> p (a c) d", d=D),
                  adj_in[0][:, 2:4, :].rearrange("p a (c d) -> p (a c) d", d=D), h0[0][:, :, :]]

        p_r = pb("p_r", [128, COLS])
        p_z = pb("p_z", [128, COLS])
        p_in = pb("p_in", [128, COLS])
        p_hn = pb("p_hn", [128, COLS])
        p_agg = [pb(f"p_agg{i}", [128, COLS]) for i in range(2)]
        p_y = pb("p_y", [128, COLS])
        p_s = pb("p_s", [128, COLS])
        p_last = [p_y, p_s, p_y, p_r]
        p_v = [p_agg[1][:, 0:G3], p_in[:, 0:G3], p_y[:, 0:G3], p_s[:, COLS - G3:COLS], p_y[:, 0:G3]]

        s_small_in = sem("small_in")
        s_w_in = [sem(f"w_in{i}") for i in range(3)]
        s_x_in = [sem(f"x_in{i}") for i in range(2)]
        s_adj_in = sem("adj_in_sem")
        s_out = [sem(f"out_sent{i}") for i in range(2)]
        s_out_last = [sem(f"last_out_sent{i}") for i in range(len(LAST))]
        s_pool_own = sem("pool_own")
        s_ident = sem("ident_ready")
        s_ones = sem("ones_ready")
        s_dve_own = sem("dve_own")
        s_pe_setup = sem("pe_setup")
        s_setup_used = sem("setup_used")
        s_whi = sem("weights_hi")
        s_weights = sem("weights_ready")
        s_scales = sem("scales_ready")
        s_bias = sem("bias_ready")
        s_stats_own = sem("stats_own")
        s_moments = sem("moments_ready")
        s_var = sem("var_ready")
        s_rstd = sem("rstd_ready")
        s_shift = sem("shift_ready")
        s_x0 = sem("h0_ready")
        s_h0hi = sem("h0_hi_ready")
        s_h0lo = sem("h0_lo_ready")
        s_ht0 = sem("hT0_ready")
        s_h0 = sem("h0_in_h")
        s_a = sem("a_ready")
        s_agg = sem("agg_done")
        s_agghi = sem("agg_hi_ready")
        s_agglo = sem("agg_lo_ready")
        s_pr = sem("p_r_done")
        s_pz = sem("p_z_done")
        s_pin = sem("p_in_done")
        s_r = sem("r_ready")
        s_z = sem("z_ready")
        s_t = sem("t_ready")
        s_u = sem("u_ready")
        s_n = sem("n_ready")
        s_v = sem("v_own")
        s_zh = sem("zh_ready")
        s_hnew = sem("h_new_ready")
        s_hi = sem("hi_ready")
        s_lo = sem("lo_ready")
        s_hn = [sem(f"hN_ready{i}") for i in range(2)]
        s_ty = sem("ty_done")
        s_ysum = sem("y_summed")
        s_ym = sem("y_masked")
        s_y = sem("y_ready")
        s_yd = sem("y_direct_ready")

        block = ctx.enter_context(nc.Block())

        OWN_MAX, OWN_TOP = 1, 8

        def wait(eng, s, count):
            if isinstance(count, int) and count <= 0:
                return
            eng.wait_ge(s, count)

        def group(k):
            return k // GSTEPS

        def slot(s, k):
            return (s & (GP - 1)) + GP * group(k)

        def half(s):
            return s >> 1

        def real(k):
            return 0 <= k < STEPS

        def split(k):
            return real(k) and k < STEPS - DIRECT

        def cuts(k):
            if k == STEPS - 1:
                return [(0, slice(0, N)), (1, slice(N, COLS))]
            return [(0, slice(0, COLS))]

        def end(k):
            return real(k) and k % GSTEPS >= GLAST

        def end_count(s, k):
            return s - GLAST * (group(k) + 1)

        def first(k):
            return real(k) and k % GSTEPS < GP

        def prepared(s, k, stage):
            if -PREP + stage <= k < GP - PREP + stage:
                return s + PREP - stage, (k + PREP - stage) % 2
            start = GSTEPS * group(k) + GP
            if k >= 0 and start <= k < STEPS - GSTEPS and k % GP == stage:
                return ((s - start) >> LOG_GP) + GP * (group(k) + 1), 0
            return None

        def before(q):
            return q - 1 if isinstance(q, int) and q < GP else q

        def run(eng, step):
            for loop, a, b in STRETCHES:
                if loop:
                    with eng.Fori(a // GP, b // GP) as i:
                        for k in range(GP):
                            step(i * GP + k, a + k)
                else:
                    for s in range(a, b):
                        step(s, s)

        @block.sync
        def _(sp):
            def pair_of(q):
                return nc.s_assert_within(q, 0, PAIRS - 1, skip_runtime_bounds_check_because="the loops end there")

            def slot_of(s, k):
                if isinstance(s, int):
                    return slot(s, k)
                return pair_of(s - (s >> LOG_GP) * GP + GP * group(k))

            def to_nodes(pair):
                return sp.dma_start_transpose(hN[:, pair, :, :, :].rearrange("p t c d -> p (t c) d"),
                                              hT[:, pair, :, :].rearrange("p t c -> p (t c)"))

            def to_features(pair):
                return sp.dma_start_transpose(hT[:, pair, :, :].rearrange("p t (c q) -> p (t c) q", c=CH),
                                              hN[:, pair, :, :, :].rearrange("p t c d -> p (t c d)"))

            def load_adj(q, w):
                wait(sp, s_adj_in, 16 * q)
                wait(sp, s_a, before(q))
                sp.dma_start(adj_in[w][:, :, :], adj_v[pair_of(q)]).then_inc(s_adj_in, 16)

            def load_x(q):
                wait(sp, s_x_in[1], 16 * (q - GP + 2))
                sp.dma_start(xs[:, pair_of(q), :, :], x_v[pair_of(q)]).then_inc(s_x_in[1], 16)

            def first_parts(s, k):
                if p := prepared(s, k, 2):
                    q, _ = p
                    wait(sp, s_h0lo, q + 1)
                    wait(sp, s_ht0, 16 * q)
                    to_features(pair_of(q)).then_inc(s_ht0, 16)

            def step(s, k):
                if k >= -1 and (p := prepared(s, k, 0)):
                    load_adj(*p)
                    if GP <= k < STEPS - GSTEPS - GP:
                        load_x(p[0] + 1)
                first_parts(s, k)
                if split(k - 1):
                    o, w = s - 1, (k - 1) % 2
                    wait(sp, s_lo, o + 1)
                    wait(sp, s_hn[w], 16 * half(o))
                    to_nodes(slot_of(o, k - 1)).then_inc(s_hn[w], 16)
                if -PREP + 1 < k < -1 and (p := prepared(s, k, 0)):
                    load_adj(*p)
                if k == 0:
                    load_x(GP)
                if end(k - 3) and split(k - 3):
                    o, w = s - 3, (k - 3) % 2
                    e = end_count(o, k - 3)
                    wait(sp, s_y, e + 1)
                    sp.dma_start(out_v[slot_of(o, k - 3)], y[w].rearrange("p (c d) -> p c d", c=CH)
                                 ).then_inc(s_out[w], 16)
                for i, (o, c0, c1) in enumerate(LAST):
                    if o == k - 2:
                        wait(sp, s_yd, i + 1)
                        sp.dma_start(out_v[slot(o, o), :, c0:c1, :], y_last[o - (STEPS - DIRECT)][:, c0:c1, :]
                                     ).then_inc(s_out_last[i], 16)

            sp.dma_start(xs[:, 0, :, :], x_v[0]).then_inc(s_x_in[0], 16)
            sp.dma_start(w_raw, weight.rearrange("l d e -> d l e")).then_inc(s_w_in[2], 16)
            sp.dma_start(xs[:, 1, :, :], x_v[1]).then_inc(s_x_in[1], 16)
            load_adj(0, 0)
            sp.wait_ge(s_x_in[1], 16)
            sp.dma_start(xs[:, 2:GP, :, :].rearrange("q t c d -> q (t c) d"),
                         x_v[2:GP].rearrange("t q c d -> q (t c) d")).then_inc(s_x_in[1], 16)
            load_adj(1, 1)
            run(sp, step)
            for w in range(2):
                sp.wait_ge(s_out[w], 16 * len([e for e in range(STEPS - DIRECT) if end(e) and e % 2 == w]))
            for i in range(len(LAST)):
                sp.wait_ge(s_out_last[i], 16)

        @block.tensor
        def _(pe):
            def setup(k):
                if k == -PREP:
                    pe.wait_ge(s_ident, 1)
                    pe.wait_ge(s_w_in[0], 16)
                    for g in range(3):
                        t = nc.tensor.transpose(p_r[:, g * D:(g + 1) * D], ih_raw[:, g, :], ident[:, :])
                    t.then_inc(s_pe_setup, 1)
                    pe.wait_ge(s_w_in[2], 16)
                    for l in range(L):
                        bank = p_z if l < 4 else p_in
                        c = (l % 4) * D
                        t = nc.tensor.transpose(bank[:, c:c + D], w_raw[:, l, :], ident[:, :])
                    t.then_inc(s_pe_setup, 1)
                    pe.wait_ge(s_w_in[1], 16)
                    for g in range(3):
                        nc.tensor.transpose(p_hn[:, g * D:(g + 1) * D], hh_raw[:, g, :], ident[:, :])
                if k == -PREP + 1:
                    pe.wait_ge(s_dve_own, OWN_MAX)
                    for i in range(3):
                        t = nc.tensor.transpose(p_s[0:1, i * 128:(i + 1) * 128], w_max[:, i:i + 1], ident[:, :])
                    t.then_inc(s_pe_setup, 1)
                    pe.wait_ge(s_setup_used, 1)
                    for l in range(2):
                        nc.tensor.matmul(p_v[l], wlT[:, l, :], ihT[:, :], start=True, stop=True
                                         ).then_inc(s_pe_setup, 1)
                    pe.wait_ge(s_ones, 1)
                    pe.wait_ge(s_dve_own, OWN_TOP)
                    nc.tensor.matmul(p_s[:, 384:387], ones_row[0:1, :], top[0:1, 0:3], start=True, stop=True
                                     ).then_inc(s_pe_setup, 1)
                if k == -PREP + 2:
                    nc.tensor.matmul(p_v[2], wlT[:, 2, :], ihT[:, :], start=True, stop=True
                                     ).then_inc(s_pe_setup, 1)
                    pe.wait_ge(s_small_in, 48)
                    nc.tensor.transpose(p_z[:, 0:70], rows[:, :], ident[0:70, 0:70]
                                        ).then_inc(s_pe_setup, 1)
                if k == 2:
                    pe.wait_ge(s_weights, 3)
                    nc.tensor.matmul(p_v[4], wlT[:, 4, :], ihT[:, :], start=True, stop=True
                                     ).then_inc(s_pe_setup, 1)

            def aggregate(s, k):
                if not real(k + 1):
                    return
                a, w = s + 1, (k + 1) % 2
                pair = slot(a, k + 1)
                if first(k + 1):
                    wait(pe, s_h0lo, pair + 1)
                    wait(pe, s_a, pair + 1)
                    if k == 0:
                        pe.wait_ge(s_weights, 1)
                else:
                    wait(pe, s_hn[w], 16 * (half(a - GP) + 1))
                wait(pe, s_agglo, a - 1)
                for b in range(2):
                    for m in range(4):
                        hf, part = m // 2, m % 2
                        t = nc.tensor.matmul(p_agg[w][:, b * N:(b + 1) * N], hN[:, pair, part, 2 * b + hf, :],
                                             A[:, pair, 2 * b + hf, :], start=(m == 0), stop=(m == 3))
                t.then_inc(s_agg, 1)

            def step(s, k):
                if k < 0:
                    setup(k)
                for i, (o, c0, c1) in enumerate(LAST):
                    if o == k - 2:
                        wait(pe, s_hnew, o + 1 + (c0 > 0))
                        wait(pe, s_yd, i - 1)
                        for c in range(c0, c1):
                            t = nc.tensor.transpose(p_last[i][:, c * 128:(c + 1) * 128],
                                                    h[:, slot(o, o), c * 128:(c + 1) * 128], ident[:, :])
                        t.then_inc(s_ty, 1)
                if k < 0:
                    aggregate(s, k)
                if k == -1:
                    pe.wait_ge(s_scales, 1)
                    nc.tensor.matmul(p_v[3], wlT[:, 3, :], ihT[:, :], start=True, stop=True
                                     ).then_inc(s_pe_setup, 1)
                if real(k):
                    layer = (s - GSTEPS * group(k)) >> LOG_GP
                    pair = slot(s, k)
                    hi, lo = hT[:, pair, 0, :], hT[:, pair, 1, :]
                    ahi, alo = agg[k % 2][:, 0, :], agg[k % 2][:, 1, :]

                    def products(bank, gate, table, data, start, stop):
                        c = gate * D
                        nc.tensor.matmul(bank[:, :], table[:, 0, c:c + D], data[0], start=start, stop=False)
                        nc.tensor.matmul(bank[:, :], table[:, 0, c:c + D], data[1], start=False, stop=False)
                        return nc.tensor.matmul(bank[:, :], table[:, 1, c:c + D], data[0], start=False, stop=stop)

                    V = VT[:, layer, :, :]
                    if k == 0:
                        pe.wait_ge(s_weights, 1)
                    if k == GP:
                        pe.wait_ge(s_weights, L)
                    if first(k):
                        wait(pe, s_ht0, 16 * (pair + 1))
                    wait(pe, s_t, s)
                    products(p_hn, 2, WT, (hi, lo), True, True)
                    wait(pe, s_r, s)
                    products(p_r, 0, WT, (hi, lo), True, False)
                    wait(pe, s_agglo, s + 1)
                    products(p_r, 0, V, (ahi, alo), False, True).then_inc(s_pr, 1)
                    aggregate(s, k)
                    if k == 0:
                        pe.wait_ge(s_bias, 1)
                    wait(pe, s_z, s)
                    products(p_z, 1, WT, (hi, lo), True, False)
                    products(p_z, 1, V, (ahi, alo), False, True).then_inc(s_pz, 1)
                    setup(k)
                    if k == 0:
                        pe.wait_ge(s_weights, 2)
                    wait(pe, s_u, s)
                    products(p_in, 2, V, (ahi, alo), True, True).then_inc(s_pin, 1)

            run(pe, step)

        @block.scalar
        def _(act):
            def hi_part(l, product):
                act.wait_ge(s_pe_setup, product)
                nc.scalar.activation(VT[:, l, 0, :], p_v[l], ACT.Copy, scale=scales[:, 0:1]).then_inc(s_whi, 1)

            def setup(k):
                if k == -PREP:
                    act.dma_start(ih_raw, w_ih.rearrange("(g f) e -> f g e", g=3)).then_inc(s_w_in[0], 16)
                    act.dma_start(hh_raw, w_hh.rearrange("(g f) e -> f g e", g=3)).then_inc(s_w_in[1], 16)
                    act.wait_ge(s_ones, 1)
                    nc.scalar.activation(warm[:, :], ones_row[0:1, 0:1], ACT.Sigmoid)
                    act.dma_start(rows[0:64, :], mask_v).then_inc(s_small_in, 16)
                    act.dma_start(rows[64:67, :], b_ih.rearrange("(g f) -> g f", g=3)).then_inc(s_small_in, 16)
                    act.dma_start(rows[67:70, :], b_hh.rearrange("(g f) -> g f", g=3)).then_inc(s_small_in, 16)
                    act.wait_ge(s_pe_setup, 1)
                    nc.scalar.activation(ihT[:, :], p_r[:, 0:G3], ACT.Copy)
                    act.wait_ge(s_pe_setup, 2)
                    nc.scalar.activation(wlT[:, 0:4, :].rearrange("p l d -> p (l d)"), p_z[:, :], ACT.Copy)
                    nc.scalar.activation(wlT[:, 4, :], p_in[:, 0:D], ACT.Copy).then_inc(s_setup_used, 1)
                if k == -PREP + 3:
                    act.wait_ge(s_scales, 1)
                    nc.scalar.activation(WT[:, 0, :], p_hn[:, 0:G3], ACT.Copy, scale=scales[:, 1:2])
                    hi_part(0, 4)
                if k == 2:
                    hi_part(4, 10)

            def first_state(s, k, part):
                if p := prepared(s, k, 0 if part == 0 and k >= GP else 1):
                    q, w = p
                    if part == 0:
                        wait(act, s_shift, q + 1)
                        wait(act, s_h0lo, before(q))
                    for c in range(2 * part, 2 * part + 2):
                        t = nc.scalar.activation(h0[w][:, c, :], xs[:, q, c, :], ACT.Relu,
                                                 bias=shift[w][:, c:c + 1], scale=rstd[w][:, c:c + 1])
                    if part == 1:
                        t.then_inc(s_x0, 1)

            def step(s, k):
                if k < 0:
                    setup(k)
                if real(k - 1):
                    o = s - 1
                    for i, cols in cuts(k - 1):
                        wait(act, s_u, o + 1 + i)
                        nc.scalar.activation(n[(k - 1) % 2][:, cols], ru[(k - 1) % 2][:, cols], ACT.Tanh,
                                             bias=bias[:, 2:3], scale=scales[:, 2:3]).then_inc(s_n, 1)
                if p := prepared(s, k, 2):
                    q, w = p
                    wait(act, s_x0, q + 1)
                    nc.scalar.activation(hN[:, q, 0, :, :], h0[w][:, :, :], ACT.Copy).then_inc(s_h0hi, 1)
                if real(k):
                    if k == 0:
                        hi_part(2, 7)
                        hi_part(3, 9)
                        act.wait_ge(s_bias, 1)
                    wait(act, s_pr, s + 1)
                    wait(act, s_n, s - 1)
                    nc.scalar.activation(ru[k % 2][:, :], p_r[:, :], ACT.Sigmoid, bias=bias_r[:, :],
                                         scale=scales[:, 2:3]).then_inc(s_r, 1)
                if real(k + 1):
                    a, w = s + 1, (k + 1) % 2
                    wait(act, s_agg, a + 1)
                    wait(act, s_pin, a - 1)
                    nc.scalar.activation(agg[w][:, 0, :], p_agg[w][:, :], ACT.Copy).then_inc(s_agghi, 1)
                if k == -PREP + 3:
                    hi_part(1, 5)
                if split(k - 1):
                    o = s - 1
                    pair = slot(o, k - 1)
                    wait(act, s_hnew, o + 1)
                    nc.scalar.activation(hT[:, pair, 0, :], h[:, pair, :], ACT.Copy).then_inc(s_hi, 1)
                if real(k):
                    wait(act, s_pz, s + 1)
                    wait(act, s_hnew, s - 1)
                    nc.scalar.activation(z[k % 2][:, :], p_z[:, :], ACT.Sigmoid, bias=bias_z[:, :],
                                         scale=scales[:, 2:3]).then_inc(s_z, 1)
                if k >= 0:
                    setup(k)
                first_state(s, k, 0)
                first_state(s, k, 1)

            run(act, step)

        @block.vector
        def _(dve):
            own = [0]

            def chained(ins):
                own[0] += 1
                ins.then_inc(s_dve_own, 1)
                dve.wait_ge(s_dve_own, own[0])

            def setup(k):
                if k == -PREP:
                    dve.wait_ge(s_w_in[0], 16)
                    nc.vector.tensor_reduce(w_max[:, 0:1], ih_raw, AX.XY, ALU.max, apply_absolute_value=True)
                    dve.wait_ge(s_w_in[2], 16)
                    nc.vector.tensor_reduce(w_max[:, 1:2], w_raw, AX.XY, ALU.max, apply_absolute_value=True)
                    dve.wait_ge(s_w_in[1], 16)
                    chained(nc.vector.tensor_reduce(w_max[:, 2:3], hh_raw, AX.XY, ALU.max, apply_absolute_value=True))
                    assert own[0] == OWN_MAX
                if k == -PREP + 1:
                    dve.wait_ge(s_pe_setup, 3)
                    chained(nc.vector.tensor_reduce(top[:, 4:7], p_s[0:1, 0:384].rearrange("p (i c) -> p i c", i=3),
                                                    AX.X, ALU.max))
                    chained(nc.vector.tensor_scalar(top[:, 4:5], top[:, 4:5], float(D), top[:, 5:6],
                                                    ALU.mult, ALU.mult))
                    chained(nc.vector.tensor_tensor(top[:, 3:4], top[:, 4:5], top[:, 6:7], ALU.max))
                    chained(nc.vector.tensor_scalar(top[:, 3:4].bitcast(I32), top[:, 3:4].bitcast(I32), 0x7F800000,
                                                    None, ALU.bitwise_and))
                    chained(nc.vector.tensor_scalar(top[:, 3:4], top[:, 3:4], 2.0 ** -60, 2.0 ** 100,
                                                    ALU.max, ALU.min))
                    chained(nc.vector.reciprocal(top[:, 7:8], top[:, 3:4]))
                    nc.vector.tensor_scalar(top[:, 2:3], top[:, 3:4], 1.0 / (S_V * S_AGG), None, ALU.mult)
                    nc.vector.tensor_scalar(top[:, 1:2], top[:, 7:8], S_V * S_AGG / S_H, None, ALU.mult)
                    chained(nc.vector.tensor_scalar(top[:, 0:1], top[:, 7:8], S_V, None, ALU.mult))
                    assert own[0] == OWN_TOP
                if k == -1:
                    dve.wait_ge(s_pe_setup, 8)
                    nc.vector.tensor_scalar(mask_t[:, :], p_z[:, 0:64], 1.0 / S_H, None, ALU.mult)
                    chained(nc.vector.tensor_copy(bias[:, :], p_z[:, 64:70]))
                    nc.vector.tensor_tensor(bias_r[:, :], bias[:, 0:1], bias[:, 3:4], ALU.add)
                    nc.vector.tensor_tensor(bias_z[:, :], bias[:, 1:2], bias[:, 4:5], ALU.add)
                    nc.vector.tensor_scalar(bias_hn[:, :], bias[:, 5:6], scales[:, 0:1], S_AGG, ALU.mult, ALU.mult
                                            ).then_inc(s_bias, 1)
                if k == 0:
                    dve.wait_ge(s_whi, 2)
                    nc.vector.scalar_tensor_tensor(VT[:, 1, 1, :], p_v[1], scales[:, 0:1], VT[:, 1, 0, :],
                                                   ALU.mult, ALU.subtract).then_inc(s_weights, 1)
                if 1 <= k < L - 1:
                    l = k + 1
                    dve.wait_ge(s_whi, 1 + l)
                    nc.vector.scalar_tensor_tensor(VT[:, l, 1, :], p_v[l], scales[:, 0:1], VT[:, l, 0, :],
                                                   ALU.mult, ALU.subtract).then_inc(s_weights, 1)

            def result_parts(s, k):
                if end(k - 3) and split(k - 3):
                    o, w = s - 3, (k - 3) % 2
                    e = end_count(o, k - 3)
                    wait(dve, s_hn[w], 16 * (half(o) + 1))
                    wait(dve, s_out[w], 16 * half(e))
                    parts = hN[:, slot(o, k - 3), :, :, :].rearrange("p t c d -> p t (c d)")
                    nc.vector.tensor_tensor(y[w], parts[:, 0, :], parts[:, 1, :], ALU.add).then_inc(s_ysum, 1)

            def masked(s, k):
                if end(k - 3) and split(k - 3):
                    o, w = s - 3, (k - 3) % 2
                    wait(dve, s_ysum, end_count(o, k - 3) + 1)
                    y_chunks = y[w].rearrange("p (c d) -> p c d", c=CH)
                    nc.vector.tensor_tensor(y_chunks, y_chunks,
                                            mask_t[:, bass.ds(slot(o, k - 3) * CH, CH)].unsqueeze(2)
                                            .to_broadcast([128, CH, D]), ALU.mult).then_inc(s_ym, 1)

            def direct_result(k):
                for i, (o, c0, c1) in enumerate(LAST):
                    if o == k - 2:
                        pair = slot(o, o)
                        wait(dve, s_ty, i + 1)
                        for c in range(c0, c1):
                            m = pair * CH + c
                            t = nc.vector.scalar_tensor_tensor(
                                y_last[o - (STEPS - DIRECT)][:, c, :], p_last[i][:, c * D:(c + 1) * D],
                                mask_t[:, m:m + 1], xs[:, pair, c, :], ALU.mult, ALU.add)
                        t.then_inc(s_yd, 1)

            def moments_of(s, k):
                if p := prepared(s, k, 0):
                    q, w = p
                    for c in range(CH):
                        t = nc.vector.bn_aggr(moments[w][:, c, :], stats[w][:, c, :])
                    t.then_inc(s_moments, 1)
                    wait(dve, s_moments, q + 1)
                    wait(dve, s_shift, before(q))
                    nc.vector.tensor_scalar(var_s[w][:, :], moments[w][:, :, 1], EPS, 1.0 / S_H ** 2,
                                            ALU.add, ALU.mult)
                    nc.vector.tensor_scalar(minus_mean[w][:, :], moments[w][:, :, 0], -1.0, None, ALU.mult
                                            ).then_inc(s_var, 1)

            def aggregated_lo(s, k):
                if real(k + 1):
                    a, w = s + 1, (k + 1) % 2
                    wait(dve, s_agghi, a + 1)
                    nc.vector.tensor_tensor(agg[w][:, 1, :], p_agg[w][:, :], agg[w][:, 0, :], ALU.subtract
                                            ).then_inc(s_agglo, 1)

            def adjacency_tile(s, k):
                if p := prepared(s, k, 1 if k < GP else 2):
                    q, w = p
                    wait(dve, s_adj_in, 16 * (q + 1))
                    nc.vector.tensor_scalar(A[:, q, :, :], adj_in[w][:, :, :], 0.0, S_A,
                                            ALU.not_equal, ALU.mult).then_inc(s_a, 1)

            def minus_n(s, k, i, cols):
                o, w = s - 1, (k - 1) % 2
                wait(dve, s_n, o + 1 + i)
                nc.vector.scalar_tensor_tensor(n[w][:, cols], z[w][:, cols], 1.0, n[w][:, cols],
                                               ALU.subtract, ALU.mult).then_inc(s_v, 1)

            def new_state(s, k, i, cols):
                o, w = s - 1, (k - 1) % 2
                wait(dve, s_v, o + 1 + i)
                wait(dve, s_zh, o + 1)
                nc.vector.scalar_tensor_tensor(h[:, slot(o, k - 1), cols], n[w][:, cols], -S_H, zh[w][:, cols],
                                               ALU.mult, ALU.add).then_inc(s_hnew, 1)

            def step(s, k):
                if k < 0:
                    aggregated_lo(s, k)
                if real(k - 1):
                    o, w = s - 1, (k - 1) % 2
                    wait(dve, s_pin, o + 1)
                    wait(dve, s_t, o + 1)
                    for _, cols in cuts(k - 1):
                        nc.vector.tensor_tensor(ru[w][:, cols], ru[w][:, cols], p_in[:, cols], ALU.add).then_inc(s_u, 1)
                if p := prepared(s, k, 0):
                    q, w = p
                    if k == -PREP:
                        dve.wait_ge(s_x_in[0], 16)
                    elif k < GP:
                        wait(dve, s_x_in[1], 16 * min(q, 2))
                    else:
                        wait(dve, s_x_in[1], 16 * (q - GP + 3))
                    for c in range(CH):
                        t = nc.vector.bn_stats(stats[w][:, c, :], xs[:, q, c, :])
                    t.then_inc(s_stats_own, 1)
                    wait(dve, s_stats_own, q + 1)
                if k == -PREP + 2:
                    dve.wait_ge(s_whi, 1)
                    nc.vector.scalar_tensor_tensor(WT[:, 1, :], p_hn[:, 0:G3], scales[:, 1:2], WT[:, 0, :],
                                                   ALU.mult, ALU.subtract)
                    nc.vector.scalar_tensor_tensor(VT[:, 0, 1, :], p_v[0], scales[:, 0:1], VT[:, 0, 0, :],
                                                   ALU.mult, ALU.subtract).then_inc(s_weights, 1)
                if k < 0:
                    moments_of(s, k)
                if k > 0:
                    setup(k)
                result_parts(s, k)
                direct_result(k)
                if real(k - 1):
                    minus_n(s, k, *cuts(k - 1)[0])
                if k >= 0:
                    moments_of(s, k)
                masked(s, k)
                if k <= 0:
                    setup(k)
                if k < -1:
                    adjacency_tile(s, k)
                if k == -PREP + 1:
                    dve.wait_ge(s_pe_setup, 6)
                    nc.vector.tensor_copy(scales[:, :], p_s[:, 384:387]).then_inc(s_scales, 1)
                if real(k - 1):
                    new_state(s, k, *cuts(k - 1)[0])
                if k == STEPS:
                    minus_n(s, k, *cuts(k - 1)[1])
                    new_state(s, k, *cuts(k - 1)[1])
                if real(k):
                    wait(dve, s_r, s + 1)
                    nc.vector.scalar_tensor_tensor(ru[k % 2][:, :], p_hn[:, :], bias_hn[:, :], ru[k % 2][:, :],
                                                   ALU.add, ALU.mult).then_inc(s_t, 1)
                if k >= 0:
                    aggregated_lo(s, k)
                if k >= -1:
                    adjacency_tile(s, k)
                if p := prepared(s, k, 3):
                    q, _ = p
                    wait(dve, s_ht0, 16 * (q + 1))
                    nc.vector.tensor_tensor(h[:, q, :], hT[:, q, 0, :], hT[:, q, 1, :], ALU.add).then_inc(s_h0, 1)

            nc.vector.memset(ones_row[:, :], 1.0).then_inc(s_ones, 1)
            run(dve, step)

        @block.gpsimd
        def _(pool):
            nc.gpsimd.memset(minus_half[:, :], -0.5)
            nc.gpsimd.memset(ident[:, :], 0.0).then_inc(s_pool_own, 1)
            pool.wait_ge(s_pool_own, 1)
            nc.gpsimd.affine_select(out=ident[:, :], in_=ident[:, :], compare_op=ALU.not_equal, fill=1.0, base=0,
                                    pattern=[[-1, 128]], channel_multiplier=1).then_inc(s_ident, 1)

            def step(s, k):
                if p := prepared(s, k, 2):
                    q, w = p
                    wait(pool, s_h0hi, q + 1)
                    nc.gpsimd.tensor_tensor(hN[:, q, 1, :, :], h0[w][:, :, :], hN[:, q, 0, :, :], ALU.subtract
                                            ).then_inc(s_h0lo, 1)
                if p := prepared(s, k, 0):
                    q, w = p
                    wait(pool, s_var, q + 1)
                    wait(pool, s_x0, before(q))
                    nc.gpsimd.tensor_tensor(rstd[w][:, :], var_s[w][:, :], minus_half[:, :], ALU.pow
                                            ).then_inc(s_rstd, 1)
                    wait(pool, s_rstd, q + 1)
                    nc.gpsimd.tensor_tensor(shift[w][:, :], minus_mean[w][:, :], rstd[w][:, :], ALU.mult
                                            ).then_inc(s_shift, 1)
                if end(k - 3) and split(k - 3):
                    o, w = s - 3, (k - 3) % 2
                    wait(pool, s_ym, end_count(o, k - 3) + 1)
                    nc.gpsimd.tensor_tensor(y[w], y[w], xs[:, slot(o, k - 3), :, :].rearrange("p c d -> p (c d)"),
                                            ALU.add).then_inc(s_y, 1)
                if split(k - 1):
                    o = s - 1
                    pair = slot(o, k - 1)
                    wait(pool, s_hi, o + 1)
                    nc.gpsimd.tensor_tensor(hT[:, pair, 1, :], h[:, pair, :], hT[:, pair, 0, :], ALU.subtract
                                            ).then_inc(s_lo, 1)
                if real(k):
                    if first(k):
                        wait(pool, s_h0, slot(s, k) + 1)
                    wait(pool, s_z, s + 1)
                    wait(pool, s_hnew, s - 1)
                    nc.gpsimd.tensor_tensor(zh[k % 2][:, :], z[k % 2][:, :], h[:, slot(s, k), :], ALU.mult
                                            ).then_inc(s_zh, 1)
            run(pool, step)


_INS = ["x", "adj", "nodemask", "L0_gnn_weight", "L0_gnn_w_ih", "L0_gnn_w_hh", "L0_gnn_b_ih", "L0_gnn_b_hh"]


def kernel(**inputs):
    import numpy as _np
    import concourse.bacc as _bacc
    from concourse import mybir as _mybir
    from concourse.bass_utils import run_bass_kernel_spmd as _run

    nc = _bacc.Bacc("TRN2", target_bir_lowering=False, num_devices=1)
    arrays, args = {}, []
    for name in _INS:
        a = _np.ascontiguousarray(inputs[name])
        arrays[f"in_{name}"] = a
        args.append(nc.dram_tensor(f"in_{name}", a.shape, _mybir.dt.from_np(a.dtype), kind="ExternalInput").ap())
    args.append(nc.dram_tensor("out_0", (B, N, D), FP32, kind="ExternalOutput").ap())
    gnn_program(nc, *args)
    return _run(nc, [arrays], core_ids=[0]).results[0]["out_0"]
```
